# Optimizing a Trainium2 kernel written in Bass

```python
import numpy as np
import jax
import jax.numpy as jnp

def _softmax(x, axis=-1):
    return jax.nn.softmax(x, axis=axis)

def _gelu(x):
    return jax.nn.gelu(x, approximate=True)

def _silu(x):
    return jax.nn.silu(x)

def _sigmoid(x):
    return jax.nn.sigmoid(x)

def _layernorm(x, axis=-1, eps=1e-05):
    m = jnp.mean(x, axis=axis, keepdims=True)
    v = jnp.var(x, axis=axis, keepdims=True)
    return (x - m) / jnp.sqrt(v + eps)

def _scatter_add(tgt, idx, src, axis=0):
    return tgt.at[idx].add(src)

def _segment_sum(src, seg, n):
    return jax.ops.segment_sum(src, seg, n)
kernel_name = 'mk_recurrent_d1_jaxref_r8_6324bd'

def setup_inputs(seed: int=0):
    np.random.seed(seed)
    _w = jnp.asarray

    def _L0_attn_setup():
        import jax, jax.numpy as jnp
        import numpy as np
        EPS_RMS = 1e-06
        EPS_GN = 1e-05

        def rms_norm(x, w, eps=EPS_RMS):
            var = jnp.mean(x * x, axis=-1, keepdims=True)
            return w * (x * jax.lax.rsqrt(var + eps))
        key = jax.random.key(seed)
        B, T, D, H, LORA, F = (4, 256, 128, 16, 64, 512)
        dk = D // H
        ks = jax.random.split(key, 20)
        s = 0.02

        def n(k, shape, scale=s):
            return jax.random.normal(k, shape, dtype=jnp.float32) * scale
        return {'x': n(ks[0], (B, T, D), 1.0), 'ln1_w': jnp.ones((D,), jnp.float32), 'mu_r': jax.random.uniform(ks[1], (D,), jnp.float32), 'mu_k': jax.random.uniform(ks[2], (D,), jnp.float32), 'mu_v': jax.random.uniform(ks[3], (D,), jnp.float32), 'mu_w': jax.random.uniform(ks[4], (D,), jnp.float32), 'mu_g': jax.random.uniform(ks[5], (D,), jnp.float32), 'Wr': n(ks[6], (D, D)), 'Wk': n(ks[7], (D, D)), 'Wv': n(ks[8], (D, D)), 'Wg': n(ks[9], (D, D)), 'Wo': n(ks[10], (D, D)), 'w0': n(ks[11], (D,), 0.5), 'wA': n(ks[12], (D, LORA)), 'wB': n(ks[13], (LORA, D)), 'u': n(ks[14], (H, dk), 0.5), 'gn_w': jnp.ones((H, dk), jnp.float32), 'gn_b': jnp.zeros((H, dk), jnp.float32), 'ln2_w': jnp.ones((D,), jnp.float32), 'ffn_w1': n(ks[15], (D, F)), 'ffn_w2': n(ks[16], (F, D))}
    _L0_attn_in = _L0_attn_setup()

    def _L0_ffn_setup():
        import jax, jax.numpy as jnp
        import numpy as np
        import math
        E = 16
        TOP_K = 2
        D = 128
        F = 512
        SH = 256
        key = jax.random.key(seed)
        ks = jax.random.split(key, 10)
        s = lambda k, shape, fan: jax.random.normal(k, shape, jnp.float32) / np.sqrt(fan)
        return {'x': jax.random.normal(ks[0], (32, 32, D), jnp.float32), 'gate_w': s(ks[1], (E, D), D), 'up_w': s(ks[2], (E, F, D), D), 'up_b': s(ks[3], (E, F), D), 'gw': s(ks[4], (E, F, D), D), 'gb': s(ks[5], (E, F), D), 'down_w': s(ks[6], (E, D, F), F), 'down_b': s(ks[7], (E, D), F), 'sh_gate_w': s(ks[8], (SH, D), D), 'sh_up_w': s(ks[9], (SH, D), D), 'sh_down_w': s(jax.random.fold_in(key, 11), (D, SH), SH)}
    _L0_ffn_in = _L0_ffn_setup()
    _d = {'L0_attn_x': _L0_attn_in['x'], 'L0_attn_ln1_w': _L0_attn_in['ln1_w'], 'L0_attn_mu_r': _L0_attn_in['mu_r'], 'L0_attn_mu_k': _L0_attn_in['mu_k'], 'L0_attn_mu_v': _L0_attn_in['mu_v'], 'L0_attn_mu_w': _L0_attn_in['mu_w'], 'L0_attn_mu_g': _L0_attn_in['mu_g'], 'L0_attn_Wr': _L0_attn_in['Wr'], 'L0_attn_Wk': _L0_attn_in['Wk'], 'L0_attn_Wv': _L0_attn_in['Wv'], 'L0_attn_Wg': _L0_attn_in['Wg'], 'L0_attn_Wo': _L0_attn_in['Wo'], 'L0_attn_w0': _L0_attn_in['w0'], 'L0_attn_wA': _L0_attn_in['wA'], 'L0_attn_wB': _L0_attn_in['wB'], 'L0_attn_u': _L0_attn_in['u'], 'L0_attn_gn_w': _L0_attn_in['gn_w'], 'L0_attn_gn_b': _L0_attn_in['gn_b'], 'L0_attn_ln2_w': _L0_attn_in['ln2_w'], 'L0_attn_ffn_w1': _L0_attn_in['ffn_w1'], 'L0_attn_ffn_w2': _L0_attn_in['ffn_w2'], 'L0_ffn_gate_w': _L0_ffn_in['gate_w'], 'L0_ffn_up_w': _L0_ffn_in['up_w'], 'L0_ffn_up_b': _L0_ffn_in['up_b'], 'L0_ffn_gw': _L0_ffn_in['gw'], 'L0_ffn_gb': _L0_ffn_in['gb'], 'L0_ffn_down_w': _L0_ffn_in['down_w'], 'L0_ffn_down_b': _L0_ffn_in['down_b'], 'L0_ffn_sh_gate_w': _L0_ffn_in['sh_gate_w'], 'L0_ffn_sh_up_w': _L0_ffn_in['sh_up_w'], 'L0_ffn_sh_down_w': _L0_ffn_in['sh_down_w']}
    _x0 = _d['L0_attn_x']
    _d['L0_attn_x'] = jax.random.normal(jax.random.fold_in(jax.random.key(seed), 1), (2, 2048, 128), dtype=_x0.dtype)
    del _x0
    return _d

def reference(L0_attn_x, L0_attn_ln1_w, L0_attn_mu_r, L0_attn_mu_k, L0_attn_mu_v, L0_attn_mu_w, L0_attn_mu_g, L0_attn_Wr, L0_attn_Wk, L0_attn_Wv, L0_attn_Wg, L0_attn_Wo, L0_attn_w0, L0_attn_wA, L0_attn_wB, L0_attn_u, L0_attn_gn_w, L0_attn_gn_b, L0_attn_ln2_w, L0_attn_ffn_w1, L0_attn_ffn_w2, L0_ffn_gate_w, L0_ffn_up_w, L0_ffn_up_b, L0_ffn_gw, L0_ffn_gb, L0_ffn_down_w, L0_ffn_down_b, L0_ffn_sh_gate_w, L0_ffn_sh_up_w, L0_ffn_sh_down_w):

    def _L0_attn_ref(x, ln1_w, mu_r, mu_k, mu_v, mu_w, mu_g, Wr, Wk, Wv, Wg, Wo, w0, wA, wB, u, gn_w, gn_b, ln2_w, ffn_w1, ffn_w2):
        import jax, jax.numpy as jnp
        import numpy as np
        EPS_RMS = 1e-06
        EPS_GN = 1e-05

        def rms_norm(x, w, eps=EPS_RMS):
            var = jnp.mean(x * x, axis=-1, keepdims=True)
            return w * (x * jax.lax.rsqrt(var + eps))
        B, T, D = x.shape
        H, dk = u.shape
        h = rms_norm(x, ln1_w)
        xx = jnp.pad(h[:, :-1], ((0, 0), (1, 0), (0, 0))) - h
        xr = h + xx * mu_r
        xk = h + xx * mu_k
        xv = h + xx * mu_v
        xw = h + xx * mu_w
        xg = h + xx * mu_g
        r = (xr @ Wr).reshape(B, T, H, dk)
        k = (xk @ Wk).reshape(B, T, H, dk)
        v = (xv @ Wv).reshape(B, T, H, dk)
        g = jax.nn.silu(xg @ Wg)
        w = w0 + jnp.tanh(xw @ wA) @ wB
        decay = jnp.exp(-jnp.exp(w)).reshape(B, T, H, dk)
        rT = jnp.moveaxis(r, 1, 0)
        kT = jnp.moveaxis(k, 1, 0)
        vT = jnp.moveaxis(v, 1, 0)
        dT = jnp.moveaxis(decay, 1, 0)

        def step(S, inps):
            rt, kt, vt, dt = inps
            kv = kt[..., :, None] * vt[..., None, :]
            o = jnp.einsum('bhk,bhkv->bhv', rt, S + u[None, :, :, None] * kv)
            S = dt[..., None] * S + kv
            return (S, o)
        S0 = jnp.zeros((B, H, dk, dk), x.dtype)
        _, oT = jax.lax.scan(step, S0, (rT, kT, vT, dT))
        o = jnp.moveaxis(oT, 0, 1)
        mean = jnp.mean(o, axis=-1, keepdims=True)
        var = jnp.var(o, axis=-1, keepdims=True)
        o = (o - mean) * jax.lax.rsqrt(var + EPS_GN) * gn_w + gn_b
        o = (o * g.reshape(B, T, H, dk)).reshape(B, T, D)
        x = x + o @ Wo
        h2 = rms_norm(x, ln2_w)
        x = x + jax.nn.gelu(h2 @ ffn_w1, approximate=False) @ ffn_w2
        return x

    def _L0_ffn_ref(x, gate_w, up_w, up_b, gw, gb, down_w, down_b, sh_gate_w, sh_up_w, sh_down_w):
        import jax, jax.numpy as jnp
        import numpy as np
        import math
        E = 16
        TOP_K = 2
        D = 128
        F = 512
        SH = 256
        B, S, Dm = x.shape
        h = x.reshape(-1, Dm)
        T = h.shape[0]
        scores = jax.nn.sigmoid(h @ gate_w.T)
        cap = math.ceil(T / E * TOP_K)
        topk_score, topk_ids = jax.lax.top_k(scores.T, cap)
        xin = h[topk_ids]
        up = jnp.einsum('ecd,efd->ecf', xin, up_w) + up_b[:, None, :]
        g = jnp.einsum('ecd,efd->ecf', xin, gw) + gb[:, None, :]
        eo = jax.nn.silu(g) * up
        eo = jnp.einsum('ecf,edf->ecd', eo, down_w) + down_b[:, None, :]
        flat = (eo * topk_score[..., None]).reshape(-1, Dm)
        out = jnp.zeros_like(h).at[topk_ids.reshape(-1)].add(flat)
        out = out.reshape(B, S, Dm)
        shared = jax.nn.silu(jnp.einsum('bsd,fd->bsf', x, sh_gate_w)) * jnp.einsum('bsd,fd->bsf', x, sh_up_w)
        shared = jnp.einsum('bsf,df->bsd', shared, sh_down_w)
        return out + shared
    x = L0_attn_x
    xn = _layernorm(x, axis=-1)
    s = _L0_attn_ref(xn, L0_attn_ln1_w, L0_attn_mu_r, L0_attn_mu_k, L0_attn_mu_v, L0_attn_mu_w, L0_attn_mu_g, L0_attn_Wr, L0_attn_Wk, L0_attn_Wv, L0_attn_Wg, L0_attn_Wo, L0_attn_w0, L0_attn_wA, L0_attn_wB, L0_attn_u, L0_attn_gn_w, L0_attn_gn_b, L0_attn_ln2_w, L0_attn_ffn_w1, L0_attn_ffn_w2)
    g = _silu(_L0_ffn_ref(xn, L0_ffn_gate_w, L0_ffn_up_w, L0_ffn_up_b, L0_ffn_gw, L0_ffn_gb, L0_ffn_down_w, L0_ffn_down_b, L0_ffn_sh_gate_w, L0_ffn_sh_up_w, L0_ffn_sh_down_w))
    x = x + s * g
    return x

_drawn_inputs = setup_inputs


def setup_inputs(seed=0):
    import zlib

    import numpy as np

    out = dict(_drawn_inputs(seed))
    spreads = {'L0_attn_ln1_w': (1.0, 0.6),
     'L0_attn_gn_w': (1.0, 0.6),
     'L0_attn_gn_b': (0.0, 0.8),
     'L0_attn_ln2_w': (1.0, 0.6)}
    factors = {'L0_attn_mu_r': 8.0,
     'L0_attn_mu_k': 8.0,
     'L0_attn_mu_v': 8.0,
     'L0_attn_mu_w': 8.0,
     'L0_attn_mu_g': 8.0,
     'L0_attn_Wr': 6.039,
     'L0_attn_Wk': 5.941,
     'L0_attn_Wv': 6.008,
     'L0_attn_Wg': 6.033,
     'L0_attn_Wo': 5.988,
     'L0_attn_w0': 8.0,
     'L0_attn_wA': 8.0,
     'L0_attn_wB': 8.0,
     'L0_attn_u': 8.0,
     'L0_attn_ffn_w1': 8.0,
     'L0_attn_ffn_w2': 8.0}
    for name, (base, spread) in spreads.items():
        noise = np.random.default_rng([zlib.crc32(name.encode()), seed]).standard_normal(out[name].shape)
        drawn = base * np.exp(spread * noise) if base else spread * noise
        out[name] = jnp.asarray(drawn.astype(out[name].dtype))
    for name, factor in factors.items():
        out[name] = (out[name] * factor).astype(out[name].dtype)
    return out
```

```python
from contextlib import ExitStack

import numpy as np

import concourse.bass as bass
from concourse import mybir

ALU = mybir.AluOpType
ACT = mybir.ActivationFunctionType
AX = mybir.AxisListType
F32 = mybir.dt.float32
F16 = mybir.dt.float16
I32 = mybir.dt.int32

P = 128
B, T, D = 2, 2048, 128
H, DK = 16, 8
LORA = 64
FF = 512
NF = FF // P
E, TOPK = 16, 2
SH = 256
TOK = B * T
CAP = TOK // E * TOPK
SEG = 512
NSEG = TOK // SEG
SPB = T // SEG
NB = SEG // P
NT = TOK // P
ROW = D + E
SA, SB_ = 32, 16
NBITS = 30
EPS_LN, EPS_RMS, EPS_GN = 1e-5, 1e-6, 1e-5
LN1, MU_R, MU_K, MU_V, MU_W, MU_G, W0, U, GNW, GNB, LN2, EPSG, NVEC = range(13)
MUS = (MU_R, MU_K, MU_V, MU_G, MU_W)


class Count:

    def __init__(self, sem, engine):
        self.sem, self.engine, self.n = sem, engine, 0
        self.loop = 0

    def sig(self, ins):
        ins.then_inc(self.sem, 1)
        self.n += 1

    def step(self, ins):
        self.sig(ins)
        self.engine.wait_ge(self.sem, self.n + self.loop)


def build(nc, d, out):
    ctx = ExitStack()
    with ctx:
        def sb(name, shape, dt=F32):
            return ctx.enter_context(nc.sbuf_tensor(name, shape, dt))

        def ps(name, shape, dt=F32):
            return ctx.enter_context(nc.psum_tensor(name, shape, dt))

        def sem(name):
            return ctx.enter_context(nc.semaphore(name))

        rows = nc.dram_tensor("row_table", [TOK, ROW], F32)
        moe_sum = nc.dram_tensor("moe_sum", [TOK, D], F32)
        v_dram = nc.dram_tensor("v_dram", [P, SEG], F32)
        s_dram = nc.dram_tensor("s_dram", [TOK, D], F32)
        share_dram = nc.dram_tensor("share_dram", [TOK, D], F32)

        ident = sb("ident", [P, P])
        selc = sb("selc", [P, DK, P])
        center = sb("center", [P, P])
        headmean = sb("headmean", [P, P])
        headones = sb("headones", [P, P])
        segones = sb("segones", [P, P])
        seglow = sb("seglow", [P, P])
        bits = sb("bits", [P, NBITS], I32)
        iota_a = sb("iota_a", [P, SA], F16)
        iota_b = sb("iota_b", [P, SB_], F16)
        tokval = sb("tokval", [P, NB * P], F16)
        vec = sb("vec", [P, NVEC])
        w_rkvg = sb("w_rkvg", [P, 4, P])
        w_o = sb("w_o", [P, P])
        w_a = sb("w_a", [P, LORA])
        w_b = sb("w_b", [LORA, P])
        w_f1 = sb("w_f1", [P, FF])
        w_f2 = sb("w_f2", [P, NF, P])
        gate = sb("gate", [P, E])
        sh_gu = sb("sh_gu", [P, 2, SH])
        sh_dn = sb("sh_dn", [P, 2, P])
        down_b = sb("down_b", [P, NSEG, P])
        ex_bias = sb("ex_bias", [P, 2, E * NF])

        xa = sb("xa", [P, NT, ROW])
        xnT = sb("xnT", [P, NSEG, SEG])
        hT = sb("hT", [P, NSEG, SEG + 1])
        stats = sb("stats", [P, NT, 6])
        mv = sb("mv", [P, NT, 2])
        small = sb("small", [P, 6, NT])
        idx_in = sb("idx_in", [P, 2, NB], I32)
        idx_out = sb("idx_out", [P, 2, NB], I32)
        minus_half = sb("minus_half", [P, NT])
        selscore = sb("selscore", [P, SEG])
        cur = sb("cur", [P, 1])
        cand = sb("cand", [P, 1])
        kept = sb("kept", [P, 1])
        cnt = sb("cnt", [P, 4])
        lim = sb("lim", [P, 2])
        idx = sb("idx", [P, (E + 1) * NB], I32)

        ARENA = 21184
        arena = sb("arena", [P, ARENA])
        used = [0]

        def carve(*shape):
            n = int(np.prod(shape))
            ap = arena[:, used[0]:used[0] + n]
            used[0] += n
            assert used[0] <= ARENA, used[0]
            if len(shape) == 2:
                return ap.rearrange("p (a b) -> p a b", a=shape[0])
            return ap

        x_in = carve(NT, P)
        hrow = carve(NT, P)
        one_a = arena[:, 0:NB * P * SA // 2].bitcast(F16).rearrange("p (t s) -> p t s", s=SA)
        one_b = carve(NB * P * SB_ // 2).bitcast(F16).rearrange("p (t s) -> p t s", s=SB_)
        r_tmp = carve(6, SEG)
        gt, eq, eqc, sel, posc, junk = (r_tmp[:, i, :] for i in range(6))
        list_ab = carve(E // 4, SB_)
        slot_i = carve(3, NB * P).bitcast(I32)
        slot_f = carve(NB * P).bitcast(F16)
        score = carve(SEG)
        gate_pad = carve(NSEG, P)
        used[0] = 0
        vb = carve(DK, SEG)
        kvS = carve(DK, SEG + 1)
        mix = carve(5, SEG)
        r_sb, k_sb, v_sb, g_sb = (carve(SEG) for _ in range(4))
        xx, tw, ew, dec, ruk, cv, sq, og = (carve(SEG) for _ in range(8))
        x2 = carve(NB, P)
        h2 = carve(NB, P)
        h2T = carve(SEG)
        gl = carve(NF, SEG)
        ms = carve(3, NB)
        share_st = sb("share_st", [P, NB, P])
        s_st = sb("s_st", [P, NB, P])
        xg = sb("xg", [P, 2, NB, ROW])
        xinT = sb("xinT", [P, SEG])
        wx = sb("wx", [P, 2, 3, FF])
        sg = sb("sg", [P, 2, SEG])
        hid = sb("hid", [P, NF, SEG])
        y = sb("y", [P, 2, NB, P])

        zeros = hid[:, 0:2, :].rearrange("p f t -> p (f t)")

        pG = [ps(f"pG{i}", [P, SEG]) for i in range(2)]
        pU = [ps(f"pU{i}", [P, SEG]) for i in range(2)]
        pY = ps("pY", [P, SEG])
        pX = ps("pX", [P, SEG])
        pR = [ps(f"pR{i}", [P, SEG]) for i in range(2)]

        const_loads = [
            (ident[:, :], d["ident"]), (vec[:, :], d["vec"]), (gate[:, :], d["gate"]),
            (segones[:, :], d["segones"]), (seglow[:, :], d["seglow"]), (bits[:, :], d["bits"]),
            (iota_a[:, :], d["iota_a"]), (iota_b[:, :], d["iota_b"]), (tokval[:, :], d["tokval"]),
            (w_rkvg[:, :, :], d["w_rkvg"]), (w_a[:, :], d["w_a"]), (w_b[:, :], d["w_b"]),
            (selc[:, :, :], d["selc"]), (center[:, :], d["center"]), (headmean[:, :], d["headmean"]),
            (headones[:, :], d["headones"]), (w_o[:, :], d["w_o"]), (w_f1[:, :], d["w_f1"]),
            (w_f2[:, :, :], d["w_f2"]), (sh_gu[:, :, :], d["sh_gu"]), (sh_dn[:, :, :], d["sh_dn"]),
            (ex_bias[:, :, :], d["ex_bias"]),
        ]
        NCONST = len(const_loads)

        x_loaded = [sem(f"x_loaded{i}") for i in range(4)]
        consts_loaded = sem("consts_loaded")
        bias_loaded = sem("bias_loaded")
        bias_zeroed = sem("bias_zeroed")
        table_stored = sem("table_stored")
        sum_zeroed = sem("sum_zeroed")
        zero_ready = sem("zero_ready")
        var_ready = sem("var_ready")
        pow_ready = sem("pow_ready")
        xn_ready = sem("xn_ready")
        hrow_ready = sem("hrow_ready")
        xnT_made = sem("xnT_made")
        hT_made = sem("hT_made")
        xnT_ready = sem("xnT_ready")
        hT_ready = sem("hT_ready")
        gate_ready = sem("gate_ready")
        logits_ready = sem("logits_ready")
        exp_ready = sem("exp_ready")
        count_ready = sem("count_ready")
        total_ready = sem("total_ready")
        slot_ready = sem("slot_ready")
        slotT_ready = sem("slotT_ready")
        slotT_used = sem("slotT_used")
        onehot_ready = sem("onehot_ready")
        list_ready = sem("list_ready")
        list_used = sem("list_used")
        idx_made = sem("idx_made")
        idx_ready = sem("idx_ready")
        dve_done = sem("dve_done")

        def bc(ap, shape):
            return ap.to_broadcast(shape)

        with nc.Block() as block:
            @block.sync
            def _(sp):
                xv = d["x"].rearrange("(q i p) c -> q p i c", p=P, q=4)
                for q in range(4):
                    sp.dma_start(x_in[:, 8 * q:8 * q + 8, :], xv[q]).then_inc(x_loaded[q], 16)
                for dst, src in const_loads:
                    sp.dma_start(dst, src).then_inc(consts_loaded, 16)
                sp.wait_ge(bias_zeroed, 1)
                for s in range(NSEG):
                    sp.dma_start(down_b[s * E:(s + 1) * E, s, :], d["down_b"]).then_inc(bias_loaded, 16)
                sp.wait_ge(zero_ready, 1)
                mz = moe_sum[:, :].rearrange("(q p i) c -> q p (i c)", p=P, q=4)
                for q in range(4):
                    sp.dma_start(mz[q], zeros).then_inc(sum_zeroed, 16)
                sp.wait_ge(slotT_used, 2)
                rv = rows[:, :].rearrange("(q i p) c -> q p i c", p=P, q=4)
                for q in range(4):
                    sp.dma_start(rv[q], xa[:, 8 * q:8 * q + 8, :]).then_inc(table_stored, 16)
                sp.wait_ge(bias_loaded, 16 * NSEG)
                sp.wait_ge(sum_zeroed, 64)
                sp.wait_ge(table_stored, 64)

            @block.gpsimd
            def _(pool):
                nc.gpsimd.memset(zeros, 0.0).then_inc(zero_ready, 1)
                nc.gpsimd.memset(down_b[:, :, :], 0.0).then_inc(bias_zeroed, 1)
                for k in range(2):
                    pool.wait_ge(var_ready, k + 1)
                    nc.gpsimd.tensor_tensor(small[:, 2 * k + 1, :], small[:, 2 * k, :], minus_half[:, :],
                                            ALU.pow).then_inc(pow_ready, 1)

            @block.vector
            def _(v):
                link = Count(dve_done, v)
                V = nc.vector
                link.step(V.memset(minus_half[:, :], -0.5))
                link.sig(V.memset(hT[:, :, 0:1], 0.0))
                link.sig(V.memset(cur[:, :], 0.0))
                link.sig(V.memset(idx[:, :], 0))
                link.step(V.memset(gate_pad[:, :, :], 0.0))
                for q in range(4):
                    v.wait_ge(x_loaded[q], 16)
                    with v.Fori(8 * q, 8 * q + 8) as i:
                        V.bn_stats(stats[:, bass.ds(i, 1), :], x_in[:, bass.ds(i, 1), :]).then_inc(dve_done, 1)
                        link.n += 0
                link.n += NT
                v.wait_ge(dve_done, link.n)
                for i in range(NT):
                    link.sig(V.bn_aggr(mv[:, i, :], stats[:, i, :]))
                v.wait_ge(dve_done, link.n)
                mean, var = mv[:, :, 0], mv[:, :, 1]
                V.tensor_scalar(small[:, 0, :], var, EPS_LN, None, ALU.add).then_inc(var_ready, 1)
                v.wait_ge(pow_ready, 1)
                link.step(V.tensor_tensor(small[:, 4, :], var, small[:, 1, :], ALU.mult))
                link.step(V.tensor_tensor(small[:, 5, :], small[:, 4, :], small[:, 1, :], ALU.mult))
                V.tensor_scalar(small[:, 2, :], small[:, 5, :], EPS_RMS, None, ALU.add).then_inc(var_ready, 1)
                with v.Fori(0, NT) as i:
                    V.tensor_scalar(xa[:, bass.ds(i, 1), 0:D], x_in[:, bass.ds(i, 1), :],
                                    mv[:, bass.ds(i, 1), 0:1], small[:, 1, bass.ds(i, 1)],
                                    ALU.subtract, ALU.mult).then_inc(xn_ready, 1)
                v.wait_ge(consts_loaded, 16 * NCONST)
                for s in range(NSEG):
                    ins = V.tensor_copy(gate_pad[:, s, s * E:(s + 1) * E], gate[:, :])
                ins.then_inc(gate_ready, 1)
                with v.Fori(0, NSEG) as s:
                    v.wait_ge(xnT_made, s + 1)
                    V.tensor_copy(xnT[:, bass.ds(s, 1), :], pG[0][:, :]).then_inc(xnT_ready, 1)
                v.wait_ge(exp_ready, 1)
                link.step(V.tensor_scalar(junk, gt, 1.0, None, ALU.add))
                link.step(V.reciprocal(score[:, :], junk))
                per = 4
                base = link.n
                with v.Fori(0, NBITS) as j:
                    k = per * j + base
                    V.tensor_tensor(cand[:, :].bitcast(I32), cur[:, :].bitcast(I32), bits[:, bass.ds(j, 1)],
                                    ALU.bitwise_or).then_inc(dve_done, 1)
                    v.wait_ge(dve_done, k + 1)
                    V.tensor_scalar(junk, score[:, :], cand[:, :], None, ALU.is_ge, ALU.add,
                                    accum_out=cnt[:, 0:1]).then_inc(count_ready, 1)
                    v.wait_ge(total_ready, j + 1)
                    V.scalar_tensor_tensor(kept[:, :], pY[:, 0:1], CAP - 0.5, cand[:, :],
                                           ALU.is_ge, ALU.mult).then_inc(dve_done, 1)
                    v.wait_ge(dve_done, k + 2)
                    V.tensor_tensor(cur[:, :], cur[:, :], kept[:, :], ALU.max).then_inc(dve_done, 1)
                    v.wait_ge(dve_done, k + 3)
                    V.memset(kept[:, :], 0.0).then_inc(dve_done, 1)
                link.n += per * NBITS
                v.wait_ge(dve_done, link.n)
                link.sig(V.tensor_scalar(gt, score[:, :], cur[:, :], None, ALU.is_gt, ALU.add,
                                         accum_out=cnt[:, 0:1]))
                link.step(V.tensor_scalar(eq, score[:, :], cur[:, :], None, ALU.is_equal, ALU.add,
                                          accum_out=cnt[:, 1:2]))
                link.step(V.memset(junk, 1.0))
                V.tensor_tensor_scan(eqc, junk, eq, 0.0, ALU.mult, ALU.add).then_inc(count_ready, 1)
                v.wait_ge(total_ready, NBITS + 1)
                link.step(V.tensor_scalar(lim[:, 0:1], pY[:, 0:1], -1.0, float(CAP), ALU.mult, ALU.add))
                link.step(V.tensor_tensor(lim[:, 1:2], lim[:, 0:1], pY[:, 3:4], ALU.subtract))
                link.step(V.scalar_tensor_tensor(eqc, eqc, lim[:, 1:2], eq, ALU.is_le, ALU.mult))
                link.step(V.tensor_tensor(sel, eqc, gt, ALU.add))
                link.step(V.tensor_tensor_scan(posc, junk, sel, 0.0, ALU.mult, ALU.add))
                V.tensor_copy(cnt[:, 2:3], posc[:, SEG - 1:SEG]).then_inc(count_ready, 1)
                link.sig(V.tensor_tensor(selscore[:, :], sel, score[:, :], ALU.mult))
                link.step(V.scalar_tensor_tensor(eq, sel, -float(TOK), posc, ALU.mult, ALU.add))
                v.wait_ge(total_ready, NBITS + 2)
                link.step(V.tensor_scalar(lim[:, 0:1], pY[:, 4:5], TOK - 1.0, None, ALU.add))
                V.tensor_scalar(gt, eq, lim[:, 0:1], None, ALU.add).then_inc(slot_ready, 1)
                v.wait_ge(slotT_ready, 1)
                V.tensor_copy(slot_i[:, 0, :], pG[0][:, :]).then_inc(slotT_used, 1)
                for b in range(NB):
                    ins = V.tensor_copy(xa[:, :, D:ROW].rearrange("p (s b) e -> p b s e", b=NB)[:, b],
                                        pG[1][:, b * P:(b + 1) * P].rearrange("p (s e) -> p s e", e=E))
                ins.then_inc(slotT_used, 1)
                v.wait_ge(slotT_used, 1)
                link.sig(V.tensor_scalar(slot_i[:, 1, :], slot_i[:, 0, :], 4, None, ALU.logical_shift_right))
                link.step(V.tensor_scalar(slot_i[:, 2, :], slot_i[:, 0, :], SB_ - 1, None, ALU.bitwise_and))
                link.sig(V.tensor_copy(slot_f[:, 0:NB * P], slot_i[:, 1, :]))
                link.step(V.tensor_copy(slot_f[:, NB * P:2 * NB * P], slot_i[:, 2, :]))
                n = NB * P
                link.sig(V.tensor_tensor(one_a, slot_f[:, 0:n].unsqueeze(2).to_broadcast([P, n, SA]),
                                         iota_a[:, :].unsqueeze(1).to_broadcast([P, n, SA]), ALU.is_equal))
                link.step(V.tensor_tensor(one_b, slot_f[:, n:2 * n].unsqueeze(2).to_broadcast([P, n, SB_]),
                                          iota_b[:, :].unsqueeze(1).to_broadcast([P, n, SB_]), ALU.is_equal))
                V.tensor_tensor(one_b, one_b, tokval[:, :].unsqueeze(2).to_broadcast([P, n, SB_]),
                                ALU.mult).then_inc(onehot_ready, 1)
                v.wait_ge(list_ready, 1)
                for e4 in range(4):
                    rr = slice(32 * e4, 32 * e4 + 32)
                    ins = V.tensor_copy(list_ab[rr, :, :],
                                        pX[rr, 0:256].rearrange("p (g f b) -> p g f b", g=4, f=4)[:, :, e4, :])
                ins.then_inc(list_used, 1)
                v.wait_ge(idx_made, 1)
                for e4 in range(4):
                    ins = V.tensor_scalar(
                        idx[:, 0:E * NB].rearrange("p (g f q) -> p g f q", g=4, f=4)[:, :, e4, :],
                        (pG + pU)[e4][:, 0:16].rearrange("p (g q) -> p g q", g=4),
                        TOK / 2.0, None, ALU.add)
                ins.then_inc(idx_ready, 1)
                v.wait_ge(hT_ready, NSEG)
                hb = hT[:, :, :].rearrange("p (b c) t -> p b c t", b=B)
                for b in range(B):
                    ins = V.tensor_copy(hb[:, b, 1:SPB, 0], hb[:, b, 0:SPB - 1, SEG])
                link.step(ins)

            @block.scalar
            def _(act):
                A = nc.scalar
                act.wait_ge(pow_ready, 2)
                with act.Fori(0, NT) as i:
                    act.wait_ge(xn_ready, i + 1)
                    A.activation(hrow[:, bass.ds(i, 1), :], xa[:, bass.ds(i, 1), 0:D], ACT.Copy,
                                 scale=small[:, 3, bass.ds(i, 1)]).then_inc(hrow_ready, 1)
                with act.Fori(0, NSEG) as s:
                    act.wait_ge(hT_made, s + 1)
                    A.activation(hT[:, bass.ds(s, 1), 1:SEG + 1], pG[1][:, :], ACT.Copy,
                                 scale=vec[:, LN1:LN1 + 1]).then_inc(hT_ready, 1)
                act.wait_ge(logits_ready, 1)
                A.activation(gt, pX[:, :], ACT.Exp, scale=-1.0).then_inc(exp_ready, 1)

            @block.tensor
            def _(pe):
                X = nc.tensor
                pe.wait_ge(consts_loaded, 16 * NCONST)
                for s in range(NSEG):
                    pe.wait_ge(xn_ready, NB * (s + 1))
                    if s:
                        pe.wait_ge(xnT_ready, s)
                    for b in range(NB):
                        ins = X.transpose(pG[0][:, b * P:(b + 1) * P], xa[:, NB * s + b, 0:D], ident[:, :])
                    ins.then_inc(xnT_made, 1)
                    pe.wait_ge(hrow_ready, NB * (s + 1))
                    if s:
                        pe.wait_ge(hT_ready, s)
                    for b in range(NB):
                        ins = X.transpose(pG[1][:, b * P:(b + 1) * P], hrow[:, NB * s + b, :], ident[:, :])
                    ins.then_inc(hT_made, 1)
                pe.wait_ge(gate_ready, 1)
                pe.wait_ge(xnT_ready, NSEG)
                for s in range(NSEG):
                    ins = X.matmul(pX[:, :], gate_pad[:, s, :], xnT[:, s, :], start=(s == 0), stop=(s == NSEG - 1))
                ins.then_inc(logits_ready, 1)
                with pe.Fori(0, NBITS) as j:
                    pe.wait_ge(count_ready, j + 1)
                    X.matmul(pY[:, 0:1], segones[:, :], cnt[:, 0:1], start=True, stop=True).then_inc(total_ready, 1)
                pe.wait_ge(count_ready, NBITS + 1)
                X.matmul(pY[:, 0:2], segones[:, :], cnt[:, 0:2], start=True, stop=True)
                X.matmul(pY[:, 2:4], seglow[:, :], cnt[:, 0:2], start=True, stop=True).then_inc(total_ready, 1)
                pe.wait_ge(count_ready, NBITS + 2)
                X.matmul(pY[:, 4:5], seglow[:, :], cnt[:, 2:3], start=True, stop=True).then_inc(total_ready, 1)
                pe.wait_ge(slot_ready, 1)
                for b in range(NB):
                    X.transpose(pG[0][:, b * P:(b + 1) * P], gt[:, b * P:(b + 1) * P], ident[:, :])
                    ins = X.transpose(pG[1][:, b * P:(b + 1) * P], score[:, b * P:(b + 1) * P], ident[:, :])
                ins.then_inc(slotT_ready, 1)
                pe.wait_ge(onehot_ready, 1)
                for g in range(E // 4):
                    for t in range(NT):
                        c = t * E + 4 * g
                        ins = X.matmul(pX[:, 64 * g:64 * g + 64],
                                       one_a[:, c:c + 4, :].rearrange("p e s -> p (e s)"),
                                       one_b[:, c:c + 4, :].rearrange("p e s -> p (e s)"),
                                       start=(t == 0), stop=(t == NT - 1))
                ins.then_inc(list_ready, 1)
                pe.wait_ge(list_used, 1)
                pe.wait_ge(slotT_used, 2)
                for e4 in range(4):
                    rr = slice(32 * e4, 32 * e4 + 32)
                    for c in range(4):
                        ins = X.matmul((pG + pU)[e4][32 * c:32 * c + 32, 0:16], ident[rr, rr],
                                       list_ab[rr, :, :].rearrange("p g (q c) -> p c g q", c=4)[:, c],
                                       start=True, stop=True, tile_position=(32 * e4, 32 * c))
                ins.then_inc(idx_made, 1)

        zeroed = sem("zeroed")
        idx_taken = sem("idx_taken")
        v_stored = sem("v_stored")
        v_spread = sem("v_spread")
        w_loaded = [sem(f"w_loaded{i}") for i in range(2)]
        gathered = [sem(f"gathered{i}") for i in range(2)]
        scattered = sem("scattered")
        share_stored = sem("share_stored")
        s_stored = sem("s_stored")
        xx_ready = sem("xx_ready")
        mix_ready = sem("mix_ready")
        r_made = sem("r_made")
        r_free = [sem(f"r_free{i}") for i in range(2)]
        ew_ready = sem("ew_ready")
        dec_ready = sem("dec_ready")
        ruk_ready = sem("ruk_ready")
        kv_ready = sem("kv_ready")
        scan_done = sem("scan_done")
        rs_ready = sem("rs_ready")
        carried = sem("carried")
        sq_ready = sem("sq_ready")
        rstd_ready = sem("rstd_ready")
        on_ready = sem("on_ready")
        gn_ready = sem("gn_ready")
        og_ready = sem("og_ready")
        x2_ready = sem("x2_ready")
        ms_ready = sem("ms_ready")
        mse_ready = sem("mse_ready")
        mpow_ready = sem("mpow_ready")
        h2_ready = sem("h2_ready")
        s_ready = sem("s_ready")
        gu_made = sem("gu_made")
        sg_ready = sem("sg_ready")
        hid_ready = sem("hid_ready")
        xT_made = sem("xT_made")
        xT_ready = sem("xT_ready")
        y_made = sem("y_made")
        y_ready = sem("y_ready")
        share_ready = sem("share_ready")

        STEPS = 2 * NF + 2
        FIRST_STEP = (0, NF, NF + 2)
        (UR, UK, UV, UG, UA, UB, UC, UO, UVAR, UWO, UH2, UF) = range(12)
        UF2 = UF + NF
        NU = UF2 + 1
        MIX_OF_USE = {UR: 0, UK: 1, UV: 2, UG: 3, UA: 4}

        def after(engine, sem, n):
            if not (isinstance(n, int) and n == 0):
                engine.wait_ge(sem, n)

        def cols(ap, i):
            return ap[:, bass.ds(i, 1), :].rearrange("p o m -> p (o m)")

        with nc.Block() as block:
            @block.sync
            def _(sp):
                def load_expert(e, buf):
                    sp.dma_start(wx[:, buf, 0:2, :], d["ex_gu"][bass.ds(e, 1)]
                                 .rearrange("o p a f -> (o p) a f")).then_inc(w_loaded[buf], 16)
                    sp.dma_start(wx[:, buf, 2, :], d["ex_dn"][bass.ds(e, 1)]
                                 .rearrange("o p f -> (o p) f")).then_inc(w_loaded[buf], 16)

                def body(it, last):
                    after(sp, r_free[UV % 2], it * (NU // 2) + UV // 2 + 1)
                    sp.dma_start(v_dram[:, :], v_sb).then_inc(v_stored, 16)
                    after(sp, v_stored, it * 16 + 16)
                    after(sp, r_made, it * NU)
                    sp.dma_start(vb.rearrange("p v t -> p (v t)"),
                                 v_dram[:, :].rearrange("(h v) t -> h (v t)", h=H).unsqueeze(1)
                                 .to_broadcast([H, DK, DK * SEG])).then_inc(v_spread, 16)
                    rows_of = lambda t: t[bass.ds(it * SEG, SEG), :].rearrange("(b p) c -> p b c", p=P)
                    if not last:
                        after(sp, y_made, it * 3 + 1)
                        load_expert(it * 2 + 2, 0)
                    after(sp, share_ready, it + 1)
                    sp.dma_start(rows_of(share_dram), share_st[:, :, :]).then_inc(share_stored, 16)
                    if not last:
                        after(sp, y_made, it * 3 + 3)
                        load_expert(it * 2 + 3, 1)
                    after(sp, s_ready, it + 1)
                    sp.dma_start(rows_of(s_dram), s_st[:, :, :]).then_inc(s_stored, 16)

                load_expert(0, 0)
                load_expert(1, 1)
                body(0, False)
                with sp.Fori(1, NSEG - 1) as it:
                    body(it, False)
                body(NSEG - 1, True)
                after(sp, share_stored, 16 * NSEG)
                after(sp, s_stored, 16 * NSEG)

            @block.gpsimd
            def _(pool):
                G = nc.gpsimd

                def take_idx(dst, e, n):
                    G.tensor_copy(dst, idx[:, bass.ds(e * NB, NB)]).then_inc(idx_taken, 1)
                    after(pool, idx_taken, n)

                def gather(buf):
                    pool.nop(nofuse=True)
                    for q in range(NB):
                        G.indirect_dma_start(xg[:, buf, q, :], None, rows[:, :],
                                             bass.IndirectOffsetOnAxis(ap=idx_in[:, buf, q:q + 1], axis=0)
                                             ).then_inc(gathered[buf], 16)

                def scatter(e, buf):
                    after(pool, y_ready, e + 1)
                    after(pool, scattered, e * 16 * NB)
                    pool.nop(nofuse=True)
                    for q in range(NB):
                        G.indirect_dma_start(moe_sum[:, :],
                                             bass.IndirectOffsetOnAxis(ap=idx_out[:, buf, q:q + 1], axis=0),
                                             y[:, buf, q, :], None, compute_op=ALU.add).then_inc(scattered, 16)

                def body(it, last):
                    e = it * 2
                    after(pool, mix_ready, it * 5)
                    G.tensor_tensor(xx, cols(hT[:, :, 0:SEG], it), cols(hT[:, :, 1:SEG + 1], it),
                                    ALU.subtract).then_inc(xx_ready, 1)
                    after(pool, y_ready, e)
                    after(pool, gathered[1], it * 16 * NB)
                    take_idx(idx_in[:, 1, :], e + 1, it * 4 + 2)
                    gather(1)
                    after(pool, v_spread, it * 16 + 16)
                    after(pool, r_free[UK % 2], it * (NU // 2) + UK // 2 + 1)
                    after(pool, carried, it)
                    for v in range(DK):
                        G.tensor_tensor(kvS[:, v, 1:SEG + 1], vb[:, v, :], k_sb, ALU.mult).then_inc(kv_ready, 1)
                    after(pool, scattered, e * 16 * NB)
                    take_idx(idx_out[:, 0, :], e, it * 4 + 3)
                    scatter(e, 0)
                    after(pool, gathered[0], (it + 1) * 16 * NB)
                    take_idx(idx_in[:, 0, :], e + 2, it * 4 + 4)
                    if not last:
                        gather(0)
                    after(pool, mse_ready, it + 1)
                    G.tensor_tensor(ms[:, 2, :], ms[:, 1, :], minus_half[:, 0:NB], ALU.pow).then_inc(mpow_ready, 1)
                    take_idx(idx_out[:, 1, :], e + 1, it * 4 + 5)
                    scatter(e + 1, 1)

                take_idx(idx_in[:, 0, :], 0, 1)
                gather(0)
                body(0, False)
                with pool.Fori(1, NSEG - 1) as it:
                    body(it, False)
                body(NSEG - 1, True)
                after(pool, scattered, 16 * NB * E)

            @block.vector
            def _(v):
                V = nc.vector
                HU_ = NU // 2

                def hid_step(it, j, f, bias_col):
                    n = it * STEPS + j
                    after(v, sg_ready, n + 1)
                    if bias_col is None:
                        V.tensor_tensor(hid[:, f, :], pU[j % 2][:, :], sg[:, j % 2, :], ALU.mult).then_inc(hid_ready, 1)
                    else:
                        V.scalar_tensor_tensor(hid[:, f, :], pU[j % 2][:, :], ex_bias[:, 1, bass.ds(bias_col, 1)],
                                               sg[:, j % 2, :], ALU.add, ALU.mult).then_inc(hid_ready, 1)

                def scale_y(it, s):
                    e = it * 2 + s
                    after(v, y_made, it * 3 + 2 * s + 1)
                    after(v, scattered, it * 2 * 16 * NB)
                    V.tensor_tensor(y[:, s, :, :], pY[:, :].rearrange("p (b c) -> p b c", b=NB),
                                    xg[:, s, :, bass.ds(e + D, 1)].to_broadcast([P, NB, P]),
                                    ALU.mult).then_inc(y_ready, 1)

                def body(it, row_end):
                    after(v, xx_ready, it + 1)
                    for m, mu in enumerate(MUS):
                        if m == 0:
                            after(v, r_made, it * NU)
                        V.scalar_tensor_tensor(mix[:, m, :], xx, vec[:, mu:mu + 1], cols(hT[:, :, 1:SEG + 1], it),
                                               ALU.mult, ALU.add).then_inc(mix_ready, 1)
                    after(v, r_free[0], it * HU_ + UR // 2 + 1)
                    after(v, r_free[1], it * HU_ + UK // 2 + 1)
                    V.scalar_tensor_tensor(ruk, r_sb, vec[:, U:U + 1], k_sb, ALU.mult, ALU.mult).then_inc(ruk_ready, 1)
                    after(v, y_made, it * 3)
                    for f in range(NF):
                        hid_step(it, FIRST_STEP[0] + f, f, it * 2 * NF + f)
                    scale_y(it, 0)
                    after(v, r_made, it * NU + UC + 1)
                    V.tensor_tensor(cv, pR[UC % 2][:, :], v_sb, ALU.mult).then_inc(r_free[UC % 2], 1)
                    after(v, y_made, it * 3 + 1)
                    for f in range(2):
                        hid_step(it, FIRST_STEP[1] + f, f, None)
                    after(v, dec_ready, it + 1)
                    for i in range(DK):
                        if i == 0:
                            after(v, y_made, it * 3 + 2)
                        after(v, kv_ready, it * DK + i + 1)
                        V.tensor_tensor_scan(kvS[:, i, 1:SEG + 1], dec, kvS[:, i, 1:SEG + 1], kvS[:, i, 0:1],
                                             ALU.mult, ALU.add).then_inc(scan_done, 1)
                        if i % 2 == 1:
                            hid_step(it, FIRST_STEP[2] + i // 2, i // 2, it * 2 * NF + NF + i // 2)
                        after(v, scan_done, it * DK + i + 1)
                        V.tensor_tensor(vb[:, i, :], r_sb, kvS[:, i, 0:SEG], ALU.mult).then_inc(rs_ready, 1)
                    after(v, rs_ready, (it + 1) * DK)
                    if row_end:
                        V.memset(kvS[:, :, 0:1], 0.0).then_inc(carried, 1)
                    else:
                        V.tensor_copy(kvS[:, :, 0:1], kvS[:, :, SEG:SEG + 1]).then_inc(carried, 1)
                    scale_y(it, 1)
                    after(v, r_free[UVAR % 2], it * HU_ + UVAR // 2 + 1)
                    V.reciprocal(ew, sq).then_inc(rstd_ready, 1)
                    after(v, rstd_ready, it + 1)
                    V.tensor_tensor(cv, pR[UO % 2][:, :], ew, ALU.mult).then_inc(r_free[UO % 2], 1)
                    after(v, gn_ready, it + 1)
                    V.tensor_tensor(og, ruk, g_sb, ALU.mult).then_inc(og_ready, 1)
                    after(v, r_made, it * NU + UWO + 1)
                    V.tensor_tensor(x2, pR[UWO % 2][:, :].rearrange("p (b c) -> p b c", b=NB),
                                    xa[:, bass.ds(it * NB, NB), 0:D], ALU.add).then_inc(r_free[UWO % 2], 1)
                    after(v, r_free[UWO % 2], it * HU_ + UWO // 2 + 1)
                    for b in range(NB):
                        V.tensor_tensor_reduce(h2[:, b, :], x2[:, b, :], x2[:, b, :], 1.0, 0.0, ALU.mult, ALU.add,
                                               ms[:, 0, b:b + 1]).then_inc(ms_ready, 1)
                    after(v, ms_ready, (it + 1) * NB)
                    V.tensor_scalar(ms[:, 1, :], ms[:, 0, :], 1.0 / D, EPS_RMS, ALU.mult, ALU.add).then_inc(mse_ready, 1)
                    after(v, mpow_ready, it + 1)
                    V.tensor_tensor(h2, x2, ms[:, 2, :].unsqueeze(2).to_broadcast([P, NB, P]),
                                    ALU.mult).then_inc(h2_ready, 1)
                    after(v, r_made, it * NU + UF2 + 1)
                    after(v, s_stored, it * 16)
                    V.tensor_tensor(s_st[:, :, :], pR[UF2 % 2][:, :].rearrange("p (b c) -> p b c", b=NB), x2,
                                    ALU.add).then_inc(r_free[UF2 % 2], 1)
                    after(v, r_free[UF2 % 2], it * HU_ + HU_)
                    V.memset(ms[:, 0, :], 0.0).then_inc(s_ready, 1)

                V.memset(kvS[:, :, 0:1], 0.0).then_inc(zeroed, 1)
                after(v, zeroed, 1)
                body(0, False)
                with v.Fori(1, SPB - 1) as it:
                    body(it, False)
                body(SPB - 1, True)
                with v.Fori(SPB, NSEG) as it:
                    body(it, False)

            @block.scalar
            def _(act):
                A = nc.scalar
                HU_ = NU // 2

                def evac(it, u, out, func, **kw):
                    after(act, r_made, it * NU + u + 1)
                    return A.activation(out, pR[u % 2][0:out.shape[0], :], func, **kw).then_inc(r_free[u % 2], 1)

                def silu_step(it, j, bias_col):
                    n = it * STEPS + j
                    after(act, gu_made, n + 1)
                    kw = {} if bias_col is None else {"bias": ex_bias[:, 0, bass.ds(bias_col, 1)]}
                    A.activation(sg[:, j % 2, :], pG[j % 2][:, :], ACT.Silu, **kw).then_inc(sg_ready, 1)

                def xT_evac(it, s):
                    after(act, xT_made, it * 2 + s + 1)
                    A.activation(xinT[:, :], pX[:, :], ACT.Copy).then_inc(xT_ready, 1)

                def body(it):
                    after(act, carried, it)
                    after(act, og_ready, it)
                    evac(it, UR, r_sb, ACT.Copy)
                    evac(it, UK, k_sb, ACT.Copy)
                    after(act, v_stored, it * 16)
                    evac(it, UV, v_sb, ACT.Copy)
                    evac(it, UG, g_sb, ACT.Silu)
                    evac(it, UA, tw[0:LORA, :], ACT.Tanh)
                    evac(it, UB, ew, ACT.Exp, bias=vec[:, W0:W0 + 1])
                    after(act, r_free[UB % 2], it * HU_ + UB // 2 + 1)
                    A.activation(dec, ew, ACT.Exp, scale=-1.0).then_inc(dec_ready, 1)
                    xT_evac(it, 0)
                    for f in range(NF):
                        silu_step(it, FIRST_STEP[0] + f, it * 2 * NF + f)
                    for f in range(2):
                        silu_step(it, FIRST_STEP[1] + f, None)
                    after(act, y_made, it * 3 + 2)
                    after(act, share_stored, it * 16)
                    A.activation(share_st[:, :, :], pY[:, :].rearrange("p (b c) -> p b c", b=NB),
                                 ACT.Copy).then_inc(share_ready, 1)
                    xT_evac(it, 1)
                    for f in range(NF):
                        silu_step(it, FIRST_STEP[2] + f, it * 2 * NF + NF + f)
                    after(act, r_made, it * NU + UO + 1)
                    A.activation(sq, pR[UO % 2][:, :], ACT.Square).then_inc(sq_ready, 1)
                    after(act, r_made, it * NU + UVAR + 1)
                    A.activation(sq, pR[UVAR % 2][:, :], ACT.Sqrt, bias=vec[:, EPSG:EPSG + 1]
                                 ).then_inc(r_free[UVAR % 2], 1)
                    after(act, r_free[UO % 2], it * HU_ + UO // 2 + 1)
                    A.activation(ruk, cv, ACT.Identity, scale=vec[:, GNW:GNW + 1],
                                 bias=vec[:, GNB:GNB + 1]).then_inc(gn_ready, 1)
                    evac(it, UH2, h2T, ACT.Copy, scale=vec[:, LN2:LN2 + 1])
                    for f in range(NF):
                        evac(it, UF + f, gl[:, f, :], ACT.Gelu)

                body(0)
                with act.Fori(1, NSEG) as it:
                    body(it)

            @block.tensor
            def _(pe):
                X = nc.tensor
                HU_ = NU // 2

                def bank(it, u):
                    after(pe, r_free[u % 2], it * HU_ + u // 2)
                    return pR[u % 2]

                def up(it, j, gw, uw, rhs):
                    if j < 2:
                        after(pe, hid_ready, it * STEPS)
                    else:
                        after(pe, hid_ready, it * STEPS + j - 1)
                    X.matmul(pG[j % 2][:, :], gw, rhs, start=True, stop=True)
                    X.matmul(pU[j % 2][:, :], uw, rhs, start=True, stop=True).then_inc(gu_made, 1)

                def transpose_x(it, s):
                    after(pe, gathered[s], (it + 1) * 16 * NB)
                    for b in range(NB):
                        ins = X.transpose(pX[:, b * P:(b + 1) * P], xg[:, s, b, 0:D], ident[:, :])
                    ins.then_inc(xT_made, 1)
                    after(pe, w_loaded[s], (it + 1) * 32)
                    after(pe, xT_ready, it * 2 + s + 1)

                def expert_step(it, s, f):
                    up(it, FIRST_STEP[2 * s] + f, wx[:, s, 0, f * P:(f + 1) * P], wx[:, s, 1, f * P:(f + 1) * P],
                       xinT[:, :])

                def expert_down(it, s):
                    after(pe, hid_ready, it * STEPS + FIRST_STEP[2 * s] + NF)
                    if s == 0:
                        after(pe, y_ready, it * 2)
                    else:
                        after(pe, share_ready, it + 1)
                    for b in range(NB):
                        for f in range(NF):
                            ins = X.matmul(pY[:, b * P:(b + 1) * P], hid[:, f, b * P:(b + 1) * P],
                                           wx[:, s, 2, f * P:(f + 1) * P], start=(f == 0), stop=(f == NF - 1))
                    ins.then_inc(y_made, 1)

                def body(it):
                    for u, m in MIX_OF_USE.items():
                        after(pe, mix_ready, it * 5 + m + 1)
                        p = bank(it, u)
                        if u == UA:
                            X.matmul(p[0:LORA, :], w_a[:, :], mix[:, m, :], start=True, stop=True).then_inc(r_made, 1)
                        else:
                            X.matmul(p[:, :], w_rkvg[:, m, :], mix[:, m, :], start=True, stop=True).then_inc(r_made, 1)
                    p = bank(it, UB)
                    after(pe, r_free[UA % 2], it * HU_ + UA // 2 + 1)
                    X.matmul(p[:, :], w_b[:, :], tw[0:LORA, :], start=True, stop=True).then_inc(r_made, 1)
                    transpose_x(it, 0)
                    for f in range(NF):
                        expert_step(it, 0, f)
                    expert_down(it, 0)
                    p = bank(it, UC)
                    after(pe, ruk_ready, it + 1)
                    X.matmul(p[:, :], headones[:, :], ruk, start=True, stop=True).then_inc(r_made, 1)
                    for f in range(2):
                        up(it, FIRST_STEP[1] + f, sh_gu[:, 0, f * P:(f + 1) * P], sh_gu[:, 1, f * P:(f + 1) * P],
                           cols(xnT[:, :, :], it))
                    after(pe, hid_ready, it * STEPS + FIRST_STEP[1] + 2)
                    after(pe, y_ready, it * 2 + 1)
                    for b in range(NB):
                        o = pY[:, b * P:(b + 1) * P]
                        for f in range(2):
                            X.matmul(o, hid[:, f, b * P:(b + 1) * P], sh_dn[:, f, :], start=(f == 0), stop=False)
                        ins = X.matmul(o, selscore[:, b * P:(b + 1) * P], cols(down_b[:, :, :], it),
                                       start=False, stop=True)
                    ins.then_inc(y_made, 1)
                    transpose_x(it, 1)
                    p = bank(it, UO)
                    after(pe, r_free[UC % 2], it * HU_ + UC // 2 + 1)
                    X.matmul(p[:, :], center[:, :], cv, start=True, stop=False)
                    for f in range(NF):
                        expert_step(it, 1, f)
                        for i in (2 * f, 2 * f + 1):
                            after(pe, rs_ready, it * DK + i + 1)
                            ins = X.matmul(p[:, :], selc[:, i, :], vb[:, i, :], start=False, stop=(i == DK - 1))
                    ins.then_inc(r_made, 1)
                    expert_down(it, 1)
                    p = bank(it, UVAR)
                    after(pe, sq_ready, it + 1)
                    X.matmul(p[:, :], headmean[:, :], sq, start=True, stop=True).then_inc(r_made, 1)
                    p = bank(it, UWO)
                    after(pe, og_ready, it + 1)
                    for b in range(NB):
                        ins = X.matmul(p[:, b * P:(b + 1) * P], og[:, b * P:(b + 1) * P], w_o[:, :],
                                       start=True, stop=True)
                    ins.then_inc(r_made, 1)
                    p = bank(it, UH2)
                    after(pe, h2_ready, it + 1)
                    for b in range(NB):
                        ins = X.transpose(p[:, b * P:(b + 1) * P], h2[:, b, :], ident[:, :])
                    ins.then_inc(r_made, 1)
                    after(pe, r_free[UH2 % 2], it * HU_ + UH2 // 2 + 1)
                    for f in range(NF):
                        p = bank(it, UF + f)
                        X.matmul(p[:, :], w_f1[:, f * P:(f + 1) * P], h2T, start=True, stop=True).then_inc(r_made, 1)
                    p = bank(it, UF2)
                    after(pe, r_free[(UF + NF - 1) % 2], it * HU_ + (UF + NF - 1) // 2 + 1)
                    for b in range(NB):
                        for f in range(NF):
                            ins = X.matmul(p[:, b * P:(b + 1) * P], gl[:, f, b * P:(b + 1) * P], w_f2[:, f, :],
                                           start=(f == 0), stop=(f == NF - 1))
                    ins.then_inc(r_made, 1)

                body(0)
                with pe.Fori(1, NSEG) as it:
                    body(it)

        fin_loaded = [sem(f"fin_loaded{q}") for q in range(4)]
        sum_ready = sem("sum_ready")
        act_ready = sem("act_ready")
        prod_ready = sem("prod_ready")
        fin_ready = sem("fin_ready")
        out_stored = sem("out_stored")
        fin = [arena[:, i * NT * P:(i + 1) * NT * P].rearrange("p (i c) -> p i c", c=P) for i in range(4)]
        with nc.Block() as block:
            @block.sync
            def _(sp):
                view = lambda t: t.rearrange("(q i p) c -> q p i c", p=P, q=4)
                for q in range(4):
                    for k, t in enumerate((moe_sum[:, :], share_dram[:, :], s_dram[:, :], d["x"])):
                        sp.dma_start(fin[k][:, 8 * q:8 * q + 8, :], view(t)[q]).then_inc(fin_loaded[q], 16)
                for q in range(4):
                    sp.wait_ge(fin_ready, q + 1)
                    sp.dma_start(view(out)[q], fin[3][:, 8 * q:8 * q + 8, :]).then_inc(out_stored, 16)
                sp.wait_ge(out_stored, 64)

            @block.vector
            def _(v):
                for q in range(5):
                    if q < 4:
                        m, sh, s, x = (t[:, 8 * q:8 * q + 8, :] for t in fin)
                        v.wait_ge(fin_loaded[q], 64)
                        nc.vector.tensor_tensor(m, m, sh, ALU.add).then_inc(sum_ready, 1)
                    if q:
                        m, sh, s, x = (t[:, 8 * q - 8:8 * q, :] for t in fin)
                        v.wait_ge(act_ready, q)
                        nc.vector.tensor_tensor(s, s, sh, ALU.mult).then_inc(prod_ready, 1)
                        v.wait_ge(prod_ready, q)
                        nc.vector.tensor_tensor(x, x, s, ALU.add).then_inc(fin_ready, 1)

            @block.scalar
            def _(act):
                for q in range(4):
                    act.wait_ge(sum_ready, q + 1)
                    nc.scalar.activation(fin[1][:, 8 * q:8 * q + 8, :], fin[0][:, 8 * q:8 * q + 8, :],
                                         ACT.Silu).then_inc(act_ready, 1)


def shape_constants():
    f = np.float32
    k = np.arange(P)
    same_head = (k[:, None] // DK == k[None, :] // DK)
    c = {"ident": np.eye(P), "headones": same_head, "headmean": same_head / DK,
         "center": np.eye(P) - same_head / DK}
    c["selc"] = same_head[:, None, :] * ((k[None, None, :] % DK == np.arange(DK)[None, :, None]) - 1.0 / DK)
    same_expert = (k[:, None] % E == k[None, :] % E)
    c["segones"] = same_expert
    c["seglow"] = same_expert & (k[:, None] // E < k[None, :] // E)
    c = {n: np.ascontiguousarray(a, f) for n, a in c.items()}
    c["bits"] = np.ascontiguousarray(np.broadcast_to(1 << np.arange(NBITS - 1, -1, -1), (P, NBITS)), np.int32)
    c["iota_a"] = np.ascontiguousarray(np.broadcast_to(np.arange(SA), (P, SA)), np.float16)
    c["iota_b"] = np.ascontiguousarray(np.broadcast_to(np.arange(SB_), (P, SB_)), np.float16)
    blk, seg = np.meshgrid(np.arange(NB), np.arange(NSEG), indexing="ij")
    base = np.repeat((seg * SEG + blk * P).ravel(), E)
    c["tokval"] = (base[None, :] + k[:, None] - TOK // 2).astype(np.float16)
    return c


def kernel(**inputs):
    import concourse.bacc as bacc
    from concourse.bass_utils import run_bass_kernel_spmd

    a = {n: np.asarray(x) for n, x in inputs.items()}
    L = {n[len("L0_attn_"):]: x for n, x in a.items() if n.startswith("L0_attn_")}
    M = {n[len("L0_ffn_"):]: x for n, x in a.items() if n.startswith("L0_ffn_")}
    f = np.float32
    eps = np.full((P,), EPS_GN, f)
    arrays = shape_constants()
    arrays["x"] = L["x"].reshape(TOK, D)
    arrays["vec"] = np.stack([L["ln1_w"], L["mu_r"], L["mu_k"], L["mu_v"], L["mu_w"], L["mu_g"], L["w0"],
                              L["u"].reshape(P), L["gn_w"].reshape(P), L["gn_b"].reshape(P), L["ln2_w"], eps], 1)
    arrays["w_rkvg"] = np.stack([L["Wr"], L["Wk"], L["Wv"], L["Wg"]], 1)
    arrays["w_a"], arrays["w_b"], arrays["w_o"] = L["wA"], L["wB"], L["Wo"]
    arrays["w_f1"] = L["ffn_w1"]
    arrays["w_f2"] = L["ffn_w2"].reshape(NF, P, D).transpose(1, 0, 2)
    arrays["gate"] = M["gate_w"].T
    arrays["sh_gu"] = np.stack([M["sh_gate_w"].T, M["sh_up_w"].T], 1)
    arrays["sh_dn"] = M["sh_down_w"].T.reshape(2, P, D).transpose(1, 0, 2)
    arrays["down_b"] = M["down_b"]
    arrays["ex_bias"] = np.stack([M["gb"].reshape(E * NF, P).T, M["up_b"].reshape(E * NF, P).T], 1)
    arrays["ex_gu"] = np.stack([M["gw"].transpose(0, 2, 1), M["up_w"].transpose(0, 2, 1)], 2)
    arrays["ex_dn"] = M["down_w"].transpose(0, 2, 1).reshape(E, NF, P, D).transpose(0, 2, 1, 3).reshape(E, P, FF)
    arrays = {n: np.ascontiguousarray(x) for n, x in arrays.items()}

    nc = bacc.Bacc("TRN2", target_bir_lowering=False, num_devices=1)
    d = {n: nc.dram_tensor("in_" + n, x.shape, mybir.dt.from_np(x.dtype), kind="ExternalInput").ap()
         for n, x in arrays.items()}
    out = nc.dram_tensor("out", (TOK, D), F32, kind="ExternalOutput").ap()
    build(nc, d, out)
    r = run_bass_kernel_spmd(nc, [{"in_" + n: x for n, x in arrays.items()}], core_ids=[0])
    return r.results[0]["out"].reshape(B, T, D)
```

```python
from contextlib import ExitStack

import numpy as np

import concourse.bass as bass
from concourse import mybir

ALU = mybir.AluOpType
ACT = mybir.ActivationFunctionType
AX = mybir.AxisListType
F32 = mybir.dt.float32
F16 = mybir.dt.float16
I32 = mybir.dt.int32

P = 128
B, T, D = 2, 2048, 128
H, DK = 16, 8
LORA = 64
FF = 512
NF = FF // P
E, TOPK = 16, 2
SH = 256
TOK = B * T
CAP = TOK // E * TOPK
SEG = 512
NSEG = TOK // SEG
SPB = T // SEG
NB = SEG // P
NT = TOK // P
ROW = D + E
SA, SB_ = 32, 16
NBITS = 30
EPS_LN, EPS_RMS, EPS_GN = 1e-5, 1e-6, 1e-5
LN1, MU_R, MU_K, MU_V, MU_W, MU_G, W0, U, GNW, GNB, LN2, EPSG, NVEC = range(13)
MIX_R, MIX_K, MIX_V, MIX_G, MIX_W = range(5)
MUS = (MU_R, MU_K, MU_V, MU_G, MU_W)


class Count:

    def __init__(self, sem, engine):
        self.sem, self.engine, self.n = sem, engine, 0
        self.loop = 0

    def sig(self, ins):
        ins.then_inc(self.sem, 1)
        self.n += 1

    def step(self, ins):
        self.sig(ins)
        self.engine.wait_ge(self.sem, self.n + self.loop)


def build(nc, d, out):
    ctx = ExitStack()
    with ctx:
        def sb(name, shape, dt=F32):
            return ctx.enter_context(nc.sbuf_tensor(name, shape, dt))

        def ps(name, shape, dt=F32):
            return ctx.enter_context(nc.psum_tensor(name, shape, dt))

        def sem(name):
            return ctx.enter_context(nc.semaphore(name))

        rows = nc.dram_tensor("row_table", [TOK, ROW], F32)
        moe_sum = nc.dram_tensor("moe_sum", [TOK, D], F32)
        v_dram = nc.dram_tensor("v_dram", [P, SEG], F32)

        ident = sb("ident", [P, P])
        selc = sb("selc", [P, DK, P])
        center = sb("center", [P, P])
        headmean = sb("headmean", [P, P])
        headones = sb("headones", [P, P])
        segones = sb("segones", [P, P])
        seglow = sb("seglow", [P, P])
        bits = sb("bits", [P, NBITS], I32)
        tokval = sb("tokval", [P, NB * P], F16)
        iota_a = sb("iota_a", [P, SA], F16)
        vec = sb("vec", [P, NVEC])
        w_rkvg = sb("w_rkvg", [P, 4, P])
        w_o = sb("w_o", [P, P])
        w_a = sb("w_a", [P, LORA])
        w_b = sb("w_b", [LORA, P])
        w_f1 = sb("w_f1", [P, FF])
        w_f2 = sb("w_f2", [P, NF, P])
        gate = sb("gate", [P, E])
        sh_gu = sb("sh_gu", [P, 2, SH])
        sh_dn = sb("sh_dn", [P, 2, P])
        ex_bias = sb("ex_bias", [P, 2, E * NF])

        xa = sb("xa", [P, NT, ROW])
        xnT = sb("xnT", [P, NSEG, SEG])
        hT = sb("hT", [P, NSEG, SEG + 1])
        mv = sb("mv", [P, NT, 2])
        small = sb("small", [P, 6, NT])
        minus_half = sb("minus_half", [P, NT])
        cur = sb("cur", [P, 1])
        cand = sb("cand", [P, 1])
        kept = sb("kept", [P, 1])
        cnt = sb("cnt", [P, 4])
        lim = sb("lim", [P, 2])
        idx = sb("idx", [P, E * NB], I32)
        idx_e = sb("idx_e", [P, 4, NB], I32)
        ms = sb("ms", [P, 3, NB])

        def region(name, size):
            t = sb(name, [P, size])
            at = [0]

            def carve(*shape):
                n = int(np.prod(shape))
                ap = t[:, at[0]:at[0] + n]
                at[0] += n
                assert at[0] <= size, (name, at[0])
                return ap.rearrange("p (a b) -> p a b", a=shape[0]) if len(shape) == 2 else ap

            def restart():
                at[0] = 0
            return carve, restart

        carve, restart = region("state", 2 * DK * SEG + DK)
        x_in = carve(NT, P)
        hrow = carve(NT, P)
        restart()
        vb = carve(DK, SEG)
        kvS = carve(DK, SEG + 1)
        moe = vb.rearrange("p v t -> p (v t)").rearrange("p (i c) -> p i c", c=P)

        mix = sb("mix", [P, 5, SEG])
        rs = sb("rs", [P, 2, SEG])
        r_next, r_cur, k_sb, v_sb, g_next, g_cur, ew, dec, ruk, cv, og = (
            sb(n, [P, SEG])[:, :] for n in
            ("r_next", "r_cur", "k_sb", "v_sb", "g_next", "g_cur", "ew", "dec", "ruk", "cv", "og"))
        x2 = sb("x2", [P, NB, P])
        h2 = sb("h2", [P, NB, P])
        h2T = sb("h2T", [P, SEG])
        gl = sb("gl", [P, NF, SEG])

        HT = NB * P // 2
        carve, restart = region("second", 9280)
        shs = carve(2, SEG)
        shu = carve(2, SEG)
        down_b = carve(NSEG, P)
        one_a = carve(SA * HT // 2).bitcast(F16).rearrange("p (t s) -> p t s", s=SA)
        one_b = carve(SB_ * HT // 2).bitcast(F16).rearrange("p (s t) -> p s t", s=SB_)
        list_ab = carve(E // 4, SB_)
        stats = shu[:, :, :].rearrange("p a b -> p (a b)")[:, 0:NT * 6].rearrange("p (i c) -> p i c", c=6)
        gate_pad = one_a.rearrange("p t s -> p (t s)").bitcast(F32)[:, 0:NSEG * P].rearrange(
            "p (s e) -> p s e", s=NSEG)
        restart()
        wx = carve(2 * 3, FF).rearrange("p (s k) f -> p s k f", s=2)
        xg = carve(2 * NB, ROW).rearrange("p (s b) c -> p s b c", s=2)
        xinT = carve(2, SEG)
        sg = carve(2, SEG)
        hid = carve(NF, SEG)
        y = sb("y", [P, 2, NB, P])
        selscore = sb("selscore", [P, SEG])
        score = sb("score", [P, SEG])[:, :]
        tmp = sb("tmp", [P, 4, SEG])
        gt, eq, eqc, junk = (tmp[:, i, :] for i in range(4))
        sel, posc = eqc, junk
        ones1 = sb("ones1", [P, 1])
        ones_row = ones1[:, 0:1].to_broadcast([P, SEG])
        slot_i = tmp[:, 1:4, :].bitcast(I32)
        slot_f = gt.bitcast(F16)

        pG = [ps(f"pG{i}", [P, SEG]) for i in range(2)]
        pU = [ps(f"pU{i}", [P, SEG]) for i in range(2)]
        pY = ps("pY", [P, SEG])
        pO = ps("pO", [P, SEG])
        pR = [ps(f"pR{i}", [P, SEG]) for i in range(2)]

        const_loads = [
            (ident[:, :], d["ident"]), (vec[:, :], d["vec"]), (gate[:, :], d["gate"]),
            (w_rkvg[:, :, :], d["w_rkvg"]), (w_a[:, :], d["w_a"]), (w_b[:, :], d["w_b"]),
            (headones[:, :], d["headones"]), (segones[:, :], d["segones"]), (bits[:, :], d["bits"]),
            (center[:, :], d["center"]), (selc[:, :, :], d["selc"]), (sh_gu[:, :, :], d["sh_gu"]),
            (sh_dn[:, :, :], d["sh_dn"]), (headmean[:, :], d["headmean"]), (w_o[:, :], d["w_o"]),
            (w_f1[:, :], d["w_f1"]), (w_f2[:, :, :], d["w_f2"]), (seglow[:, :], d["seglow"]),
            (tokval[:, :], d["tokval"]), (iota_a[:, :], d["iota_a"]), (ex_bias[:, :, :], d["ex_bias"]),
        ]
        NFIRST = 3
        x_loaded = [sem(f"x_loaded{i}") for i in range(4)]
        first_loaded = sem("first_loaded")
        consts_loaded = sem("consts_loaded")
        bias_loaded = sem("bias_loaded")
        bias_zeroed = sem("bias_zeroed")
        edges_ready = sem("edges_ready")
        stats_ready = sem("stats_ready")
        var_ready = sem("var_ready")
        pow_ready = sem("pow_ready")
        xn_ready = sem("xn_ready")
        hrow_ready = sem("hrow_ready")
        xnT_made = sem("xnT_made")
        hT_made = sem("hT_made")
        xnT_ready = sem("xnT_ready")
        hT_ready = sem("hT_ready")
        gate_ready = sem("gate_ready")
        logits_ready = sem("logits_ready")
        exp_ready = sem("exp_ready")

        def after(engine, sem, n):
            if not (isinstance(n, int) and n <= 0):
                engine.wait_ge(sem, n)
                if engine is nc.sync and not isinstance(n, int):
                    engine.nop(nofuse=True)

        def cols(ap, i):
            return ap[:, bass.ds(i, 1), :].rearrange("p o m -> p (o m)")

        QT = NT // 4
        POWERS = ((0, 0), (1, 0), (0, 1), (2, 0), (1, 1), (3, 0), (2, 1), (3, 1))

        def power(q, half):
            return POWERS.index((q, half)) + 1

        names = ("R", "K", "V", "A", "B", "C", "G", "O", "VAR", "WO", "H2", "F", "FO")
        made = {n: sem(f"{n}_made") for n in names}
        taken = {n: sem(f"{n}_taken") for n in names}
        BANK = {"VAR": 1, "R": 0, "K": 1, "V": 0, "A": 1, "B": 0, "WO": 1, "C": 0, "G": 1, "H2": 0, "FO": 1}
        F_BANK = (1, 0, 1, 0)
        xx = sb("xx", [P, SEG])[:, :]
        zeroed = sem("zeroed")
        xx_ready = sem("xx_ready")
        mix_ready = sem("mix_ready")
        v_stored = sem("v_stored")
        v_spread = sem("v_spread")
        carried = sem("carried")
        kv_ready = sem("kv_ready")
        dec_made = sem("dec_made")
        dec_ready = sem("dec_ready")
        rcur_ready = sem("rcur_ready")
        gcur_ready = sem("gcur_ready")
        ruk_ready = sem("ruk_ready")
        scan_done = sem("scan_done")
        rs_ready = sem("rs_ready")
        rs_used = sem("rs_used")
        sq_ready = sem("sq_ready")
        rstd_ready = sem("rstd_ready")
        gn_ready = sem("gn_ready")
        og_ready = sem("og_ready")
        ms_ready = sem("ms_ready")
        mse_ready = sem("mse_ready")
        mpow_ready = sem("mpow_ready")
        h2_ready = sem("h2_ready")
        search = sem("search")
        count_ready = sem("count_ready")
        total_ready = sem("total_ready")
        route = sem("route_done")
        slot_ready = sem("slot_ready")
        slotT_ready = sem("slotT_ready")
        slotT_used = sem("slotT_used")
        onehot_ready = sem("onehot_ready")
        onehot_used = sem("onehot_used")
        list_ready = sem("list_ready")
        list_used = sem("list_used")
        idx_made = sem("idx_made")
        idx_ready = sem("idx_ready")
        selscore_ready = sem("selscore_ready")
        sum_set = [sem(f"sum_set{i}") for i in range(2)]
        sh_made = sem("sh_made")
        shs_ready = sem("shs_ready")
        shu_ready = sem("shu_ready")
        shh_ready = sem("shh_ready")
        pY_made = sem("pY_made")
        pY_taken = sem("pY_taken")
        w_loaded = [sem(f"w_loaded{i}") for i in range(2)]
        gathered = [sem(f"gathered{i}") for i in range(2)]
        idx_taken = sem("idx_taken")
        dram_written = sem("dram_written")
        gu_made = sem("gu_made")
        sg_ready = sem("sg_ready")
        hid_ready = sem("hid_ready")
        xT_made = sem("xT_made")
        xT_ready = sem("xT_ready")
        y_made = sem("y_made")
        y_ready = sem("y_ready")
        x_again = sem("x_again")

        A_PASSES, LIST_PASS, LAST = range(3), 3, NSEG - 1
        PER = NBITS // 3
        EP = 4
        F0_, FO0, HID0, Y0, YM0 = 1, 1, 2, 2, 1
        TABLE = 16 * NSEG

        with nc.Block() as block:
            @block.sync
            def _(sp):
                def load_expert(e, buf):
                    sp.dma_start(wx[:, buf, 0:2, :], d["ex_gu"][bass.ds(e, 1)]
                                 .rearrange("o p a f -> (o p) a f")).then_inc(w_loaded[buf], 16)
                    sp.dma_start(wx[:, buf, 2, :], d["ex_dn"][bass.ds(e, 1)]
                                 .rearrange("o p f -> (o p) f")).then_inc(w_loaded[buf], 16)

                def spread_v(c):
                    after(sp, taken["V"], c + 1)
                    sp.dma_start(v_dram[:, :], v_sb).then_inc(v_stored, 16)
                    after(sp, v_stored, 16 * c + 16)
                    after(sp, kv_ready, DK * c)
                    sp.dma_start(vb.rearrange("p v t -> p (v t)"),
                                 v_dram[:, :].rearrange("(h v) t -> h (v t)", h=H).unsqueeze(1)
                                 .to_broadcast([H, DK, DK * SEG])).then_inc(v_spread, 16)

                def reload_x(p):
                    c = p * 2 - 8
                    for k in range(2):
                        if isinstance(p, int) and p == LAST and k == 1:
                            after(sp, taken["WO"], NSEG)
                        sp.dma_start(xa[:, bass.ds(c * NB + k * NB, NB), 0:D],
                                     d["x"][bass.ds(c * SEG + k * SEG, SEG), :]
                                     .rearrange("(b p) c -> p b c", p=P)).then_inc(x_again, 16)

                def experts(p, last):
                    for s in range(EP):
                        e = p * EP - 4 * EP + s
                        if not (last and s >= 2):
                            after(sp, y_made, e + 1 + YM0)
                            load_expert(e + 2, s % 2)

                xv = d["x"].rearrange("(q i p) c -> q p i c", p=P, q=4)
                for q in range(4):
                    sp.dma_start(x_in[:, QT * q:QT * q + QT, :], xv[q]).then_inc(x_loaded[q], 16)
                for i, (dst, src) in enumerate(const_loads):
                    sp.dma_start(dst, src).then_inc(first_loaded if i < NFIRST else consts_loaded, 16)
                sp.wait_ge(bias_zeroed, 1)
                for s in range(NSEG):
                    sp.dma_start(down_b[s * E:(s + 1) * E, s, :], d["down_b"]).then_inc(bias_loaded, 16)
                sp.wait_ge(xn_ready, NT)
                spread_v(0)
                spread_v(1)
                with sp.Fori(1, 3) as p:
                    spread_v(p + 1)
                spread_v(4)
                for c in range(NSEG):
                    sp.wait_ge(pY_taken, 8 + c)
                    sp.dma_start(moe_sum[c * SEG:(c + 1) * SEG, :].rearrange("(b p) c -> p b c", p=P),
                                 y[:, c % 2, :, :]).then_inc(sum_set[c % 2], 16)
                sp.wait_ge(list_ready, 1)
                sp.wait_ge(pY_taken, 16)
                load_expert(0, 0)
                load_expert(1, 1)
                sp.wait_ge(dram_written, TABLE)
                with sp.Fori(4, 6) as p:
                    spread_v(p + 1)
                    experts(p, False)
                    reload_x(p)
                spread_v(7)
                experts(6, False)
                reload_x(6)
                experts(7, True)
                reload_x(7)
                sp.wait_ge(x_again, 16 * NSEG)

            @block.gpsimd
            def _(pool):
                G = nc.gpsimd

                def diff(c):
                    after(pool, mix_ready, 5 * c)
                    G.tensor_tensor(xx, cols(hT[:, :, 0:SEG], c), cols(hT[:, :, 1:SEG + 1], c),
                                    ALU.subtract).then_inc(xx_ready, 1)

                def kv(c, i, carry):
                    if carry is not None:
                        after(pool, rs_ready, DK * (c - 1) + i + 1)
                    if carry == "copy":
                        pool.nop(nofuse=True)
                        G.tensor_copy(kvS[:, i, 0:1], kvS[:, i, SEG:SEG + 1]).then_inc(carried, 1)
                    else:
                        G.memset(kvS[:, i, 0:1], 0.0).then_inc(carried, 1)
                    after(pool, carried, DK * c + i + 1)
                    if i == 0:
                        after(pool, v_spread, 16 * c + 16)
                        after(pool, taken["K"], c + 1)
                    G.tensor_tensor(kvS[:, i, 1:SEG + 1], vb[:, i, :], k_sb, ALU.mult).then_inc(kv_ready, 1)

                def gate_out(c):
                    after(pool, gn_ready, c + 1)
                    after(pool, gcur_ready, c + 1)
                    G.tensor_tensor(og, og, g_cur, ALU.mult).then_inc(og_ready, 1)

                def rms_pow(c):
                    after(pool, mse_ready, c + 1)
                    G.tensor_tensor(ms[:, 2, :], ms[:, 1, :], minus_half[:, 0:NB], ALU.pow).then_inc(mpow_ready, 1)

                def gather(e, s):
                    G.tensor_copy(idx_e[:, s, :], idx[:, bass.ds(e * NB, NB)]).then_inc(idx_taken, 1)
                    pool.wait_ge(idx_taken, e + 1)
                    pool.nop(nofuse=True)
                    for q in range(NB):
                        G.indirect_dma_start(xg[:, s % 2, q, :], None, rows[:, :],
                                             bass.IndirectOffsetOnAxis(ap=idx_e[:, s, q:q + 1], axis=0)
                                             ).then_inc(gathered[s % 2], 16)

                def scatter(e, s):
                    after(pool, dram_written, e * 16 * NB + TABLE)
                    pool.nop(nofuse=True)
                    for q in range(NB):
                        G.indirect_dma_start(moe_sum[:, :],
                                             bass.IndirectOffsetOnAxis(ap=idx_e[:, s, q:q + 1], axis=0),
                                             y[:, s % 2, q, :], None, compute_op=ALU.add).then_inc(dram_written, 16)

                def store_table():
                    pool.wait_ge(slotT_used, 2)
                    rv = rows[:, :].rearrange("(q i p) c -> q p i c", p=P, q=NSEG)
                    for q in range(NSEG):
                        G.dma_start(rv[q], xa[:, NB * q:NB * q + NB, :]).then_inc(dram_written, 16)

                def first_row(p):
                    first = isinstance(p, int) and p == 0
                    diff(p + 2)
                    if not first:
                        gate_out(p - 1)
                    shared_step(p, 0, 0)
                    shared_step(p, 0, 1)
                    carry = "zero" if isinstance(p, int) and p == LIST_PASS else "copy"
                    for i in range(DK):
                        kv(p + 1, i, carry)
                        if i == 2 and not first:
                            rms_pow(p - 1)
                        if i in (4, 5):
                            shared_step(p, 1, i - 4)
                        if i == 4 and carry == "zero":
                            store_table()

                def shared_step(p, half, f):
                    n = p * 4 + 2 * half + f
                    after(pool, shs_ready, n + 1)
                    after(pool, shu_ready, n + 1)
                    G.tensor_tensor(shs[:, f, :], shs[:, f, :], shu[:, f, :], ALU.mult).then_inc(shh_ready, 1)

                def turn_over(p, s):
                    e = p * EP - 4 * EP + s
                    after(pool, y_ready, e + 1 + Y0)
                    if not (isinstance(p, int) and p == LAST and s >= 2):
                        gather(e + 2, (s + 2) % 4)
                    scatter(e, s)

                def second_row(p, mixes):
                    if mixes:
                        diff(p + 2)
                    gate_out(p - 1)
                    turn_over(p, 0)
                    for i in range(DK):
                        kv(p + 1, i, "copy")
                        if i == 2:
                            rms_pow(p - 1)
                            turn_over(p, 1)
                        if i == 5:
                            turn_over(p, 2)
                    turn_over(p, 3)

                def last_row(p):
                    for half in range(2):
                        gate_out(p - 1 + half)
                        rms_pow(p - 1 + half)
                        turn_over(p, 2 * half)
                        turn_over(p, 2 * half + 1)

                nc.gpsimd.memset(down_b, 0.0).then_inc(bias_zeroed, 1)
                for k, (q, half) in enumerate(POWERS):
                    pool.wait_ge(var_ready, k + 1)
                    G.tensor_tensor(small[:, 2 * half + 1, QT * q:QT * q + QT],
                                    small[:, 2 * half, QT * q:QT * q + QT],
                                    minus_half[:, 0:QT], ALU.pow).then_inc(pow_ready, 1)
                    if (q, half) == (2, 0):
                        pool.wait_ge(hT_ready, 1)
                        diff(0)
                pool.wait_ge(edges_ready, 1)
                diff(1)
                pool.wait_ge(hT_made, NSEG)
                for i in range(DK):
                    kv(0, i, None)
                first_row(0)
                with pool.Fori(1, 3) as p:
                    first_row(p)
                first_row(LIST_PASS)
                pool.wait_ge(idx_ready, 1)
                pool.wait_ge(dram_written, TABLE)
                for t in sum_set:
                    pool.wait_ge(t, 16 * NSEG // 2)
                pool.wait_ge(pY_taken, 16)
                gather(0, 0)
                gather(1, 1)
                with pool.Fori(4, 6) as p:
                    second_row(p, True)
                second_row(6, False)
                last_row(LAST)
                pool.wait_ge(dram_written, 16 * NB * E + TABLE)

            @block.vector
            def _(v):
                V = nc.vector

                def mixes(c, which):
                    for m in which:
                        after(v, xx_ready, c + 1)
                        after(v, made[("R", "K", "V", "G", "A")[m]], c)
                        V.scalar_tensor_tensor(mix[:, m, :], xx, vec[:, MUS[m]:MUS[m] + 1],
                                               cols(hT[:, :, 1:SEG + 1], c), ALU.mult, ALU.add).then_inc(mix_ready, 1)

                def scan(c, i):
                    after(v, kv_ready, DK * c + i + 1)
                    if i == 0:
                        after(v, dec_ready, c + 1)
                    V.tensor_tensor_scan(kvS[:, i, 1:SEG + 1], dec, kvS[:, i, 1:SEG + 1], kvS[:, i, 0:1],
                                         ALU.mult, ALU.add).then_inc(scan_done, 1)

                def r_state(c, i):
                    after(v, scan_done, DK * c + i + 1)
                    if i == 0:
                        after(v, rcur_ready, c + 1)
                    if i == 1:
                        after(v, made["O"], c)
                    else:
                        after(v, rs_used, c * (DK - 1) + max(i - 1, 0))
                    V.tensor_tensor(rs[:, i % 2, :], r_cur, kvS[:, i, 0:SEG], ALU.mult).then_inc(rs_ready, 1)

                def weigh_own(c):
                    after(v, taken["R"], c + 1)
                    after(v, taken["K"], c + 1)
                    after(v, made["C"], c)
                    V.scalar_tensor_tensor(ruk, r_next, vec[:, U:U + 1], k_sb, ALU.mult, ALU.mult).then_inc(ruk_ready, 1)

                def own(c):
                    after(v, made["C"], c + 1)
                    V.tensor_tensor(cv, pR[BANK["C"]][:, :], v_sb, ALU.mult).then_inc(taken["C"], 1)

                def normalise(c):
                    after(v, rstd_ready, c + 1)
                    V.tensor_tensor(og, pO[:, :], og, ALU.mult).then_inc(taken["O"], 1)

                def residual(c):
                    after(v, made["WO"], c + 1)
                    V.tensor_tensor(x2[:, :, :], pR[BANK["WO"]][:, :].rearrange("p (b c) -> p b c", b=NB),
                                    xa[:, bass.ds(c * NB, NB), 0:D], ALU.add).then_inc(taken["WO"], 1)
                    after(v, taken["WO"], c + 1)
                    for b in range(NB):
                        V.tensor_tensor_reduce(h2[:, b, :], x2[:, b, :], x2[:, b, :], 1.0, 0.0, ALU.mult, ALU.add,
                                               ms[:, 0, b:b + 1]).then_inc(ms_ready, 1)
                    after(v, ms_ready, c * NB + NB)
                    V.tensor_scalar(ms[:, 1, :], ms[:, 0, :], 1.0 / D, EPS_RMS, ALU.mult, ALU.add).then_inc(mse_ready, 1)

                def rms(c):
                    after(v, mpow_ready, c + 1)
                    V.tensor_tensor(h2[:, :, :], x2[:, :, :], ms[:, 2, :].unsqueeze(2).to_broadcast([P, NB, P]),
                                    ALU.mult).then_inc(h2_ready, 1)

                def block_out(c):
                    after(v, made["FO"], c + 1)
                    V.tensor_tensor(cols(hT[:, :, 0:SEG], c).rearrange("p (b c) -> p b c", b=NB),
                                    pR[BANK["FO"]][:, :].rearrange("p (b c) -> p b c", b=NB), x2[:, :, :],
                                    ALU.add).then_inc(taken["FO"], 1)

                def update(j):
                    after(v, total_ready, j)
                    V.scalar_tensor_tensor(kept[:, :], pU[1][:, 0:1], CAP - 0.5, cand[:, :],
                                           ALU.is_ge, ALU.mult).then_inc(search, 1)
                    after(v, search, j * 3 - 1)
                    V.tensor_tensor(cur[:, :], cur[:, :], kept[:, :], ALU.max).then_inc(search, 1)
                    after(v, search, j * 3)

                def search_step(j):
                    if not (isinstance(j, int) and j == 0):
                        update(j)
                    V.tensor_tensor(cand[:, :].bitcast(I32), cur[:, :].bitcast(I32), bits[:, bass.ds(j, 1)],
                                    ALU.bitwise_or).then_inc(search, 1)
                    after(v, search, j * 3 + 1)
                    V.tensor_scalar(gt, score, cand[:, :], None, ALU.is_ge, ALU.add,
                                    accum_out=cnt[:, 0:1]).then_inc(count_ready, 1)

                link = Count(route, v)

                def choose():
                    update(NBITS)
                    link.sig(V.tensor_scalar(gt, score, cur[:, :], None, ALU.is_gt, ALU.add, accum_out=cnt[:, 0:1]))
                    link.step(V.tensor_scalar(eq, score, cur[:, :], None, ALU.is_equal, ALU.add,
                                              accum_out=cnt[:, 1:2]))
                    V.tensor_tensor_scan(eqc, ones_row, eq, 0.0, ALU.mult, ALU.add).then_inc(count_ready, 1)

                def number():
                    v.wait_ge(total_ready, NBITS + 1)
                    link.step(V.tensor_scalar(lim[:, 0:1], pU[1][:, 0:1], -1.0, float(CAP), ALU.mult, ALU.add))
                    link.step(V.tensor_tensor(lim[:, 1:2], lim[:, 0:1], pU[1][:, 3:4], ALU.subtract))
                    link.step(V.scalar_tensor_tensor(eqc, eqc, lim[:, 1:2], eq, ALU.is_le, ALU.mult))
                    link.step(V.tensor_tensor(sel, eqc, gt, ALU.add))
                    link.step(V.tensor_tensor_scan(posc, ones_row, sel, 0.0, ALU.mult, ALU.add))
                    V.tensor_copy(cnt[:, 2:3], posc[:, SEG - 1:SEG]).then_inc(count_ready, 1)
                    V.tensor_tensor(selscore[:, :], sel, score, ALU.mult).then_inc(selscore_ready, 1)
                    link.step(V.scalar_tensor_tensor(eq, sel, -float(TOK), posc, ALU.mult, ALU.add))

                def place():
                    v.wait_ge(total_ready, NBITS + 2)
                    link.step(V.tensor_scalar(lim[:, 0:1], pU[1][:, 4:5], TOK - 1.0, None, ALU.add))
                    V.tensor_scalar(gt, eq, lim[:, 0:1], None, ALU.add).then_inc(slot_ready, 1)

                def turn():
                    v.wait_ge(slotT_ready, 1)
                    V.tensor_copy(slot_i[:, 0, :], pG[0][:, :]).then_inc(slotT_used, 1)
                    for b in range(NB):
                        ins = V.tensor_copy(xa[:, :, D:ROW].rearrange("p (s b) e -> p b s e", b=NB)[:, b],
                                            pG[1][:, b * P:(b + 1) * P].rearrange("p (s e) -> p s e", e=E))
                    ins.then_inc(slotT_used, 1)
                    v.wait_ge(slotT_used, 1)
                    link.sig(V.tensor_scalar(slot_i[:, 1, :], slot_i[:, 0, :], 4, None, ALU.logical_shift_right))
                    link.step(V.tensor_scalar(slot_i[:, 2, :], slot_i[:, 0, :], SB_ - 1, None, ALU.bitwise_and))
                    link.sig(V.tensor_copy(slot_f[:, 0:NB * P], slot_i[:, 1, :]))
                    link.step(V.tensor_copy(slot_f[:, NB * P:2 * NB * P], slot_i[:, 2, :]))

                def onehots(half):
                    if half:
                        v.wait_ge(onehot_used, 1)
                    t = slice(half * HT, (half + 1) * HT)
                    V.tensor_tensor(one_a, slot_f[:, t].unsqueeze(2).to_broadcast([P, HT, SA]),
                                    iota_a[:, :].unsqueeze(1).to_broadcast([P, HT, SA]), ALU.is_equal)
                    for b in range(SB_):
                        ins = V.scalar_tensor_tensor(one_b[:, b, :], slot_f[:, NB * P:2 * NB * P][:, t], float(b),
                                                     tokval[:, t], ALU.is_equal, ALU.mult)
                    ins.then_inc(onehot_ready, 1)

                def list_out():
                    v.wait_ge(list_ready, 1)
                    for e4 in range(4):
                        rr = slice(32 * e4, 32 * e4 + 32)
                        ins = V.tensor_copy(list_ab[rr, :, :],
                                            pU[1][rr, 0:256].rearrange("p (g f b) -> p g f b", g=4, f=4)[:, :, e4, :])
                    ins.then_inc(list_used, 1)

                def idx_out():
                    v.wait_ge(idx_made, 1)
                    for e4 in range(4):
                        ins = V.tensor_scalar(
                            idx[:, :].rearrange("p (g f q) -> p g f q", g=4, f=4)[:, :, e4, :],
                            (pG + pU)[e4][:, 0:16].rearrange("p (g q) -> p g q", g=4), TOK / 2.0, None, ALU.add)
                    ins.then_inc(idx_ready, 1)

                def hid_step(e, f):
                    after(v, sg_ready, e * NF + f + 1)
                    after(v, y_made, e + YM0)
                    V.scalar_tensor_tensor(hid[:, f, :], pU[f % 2][:, :], ex_bias[:, 1, bass.ds(e * NF + f, 1)],
                                           sg[:, f % 2, :], ALU.add, ALU.mult).then_inc(hid_ready, 1)

                def scale_y(e, s):
                    after(v, y_made, e + 1 + YM0)
                    after(v, dram_written, e * 16 * NB - 16 * NB + TABLE)
                    V.tensor_tensor(y[:, s % 2, :, :], pY[:, :].rearrange("p (b c) -> p b c", b=NB),
                                    xg[:, s % 2, :, bass.ds(e + D, 1)].to_broadcast([P, NB, P]),
                                    ALU.mult).then_inc(y_ready, 1)

                def column(p, i):
                    scan(p, i)
                    r_state(p, i)

                def pass_(p, searching=False, listing=False, experts=False, finish=True, mixing=True):
                    for i in range(DK):
                        e = p * EP - 4 * EP + i // 2
                        f = 2 * (i % 2)
                        for k in (((4, 5), (6,), (7,), ())[i - 4] if listing and i >= 4 else (i,)):
                            scan(p, k)
                            if searching and 1 <= i <= PER // 2:
                                search_step(p * PER + 2 * i - 2)
                            r_state(p, k)
                        if searching and 1 <= i <= PER // 2:
                            search_step(p * PER + 2 * i - 1)
                        if experts:
                            hid_step(e, f)
                            hid_step(e, f + 1)
                        if i == 0 and finish:
                            normalise(p - 1)
                        if i == 2:
                            weigh_own(p + 1)
                        if i == 3 and finish:
                            residual(p - 1)
                        if i == 4:
                            own(p + 1)
                            if finish:
                                rms(p - 1)
                        if mixing and i >= 4:
                            mixes(p + 2, ((MIX_R,), (MIX_K,), (MIX_V, MIX_G), (MIX_W,))[i - 4])
                        if listing:
                            (choose, number, place, turn, lambda: onehots(0), lambda: onehots(1), list_out, idx_out)[i]()
                        if experts and i % 2 == 1:
                            scale_y(e, i // 2)
                    if finish:
                        block_out(p - 1)

                def last_pass(p):
                    for i in range(DK):
                        e = p * EP - 4 * EP + i // 2
                        f = 2 * (i % 2)
                        c = p - 1 + i // 4
                        if i < 4:
                            column(p, 2 * i)
                        hid_step(e, f)
                        if i < 4:
                            column(p, 2 * i + 1)
                        hid_step(e, f + 1)
                        if i % 4 == 0:
                            normalise(c)
                        if i % 4 == 2:
                            residual(c)
                            rms(c)
                        if i % 2 == 1:
                            scale_y(e, i // 2)
                        if i % 4 == 3:
                            block_out(c)

                for k, (s, n) in enumerate(((taken["FO"], FO0), (hid_ready, HID0), (y_ready, Y0))):
                    V.memset(cnt[:, k:k + 1], 0.0).then_inc(s, n)
                V.memset(ones1[:, :], 1.0)
                link.sig(V.memset(minus_half[:, :], -0.5))
                link.sig(V.memset(hT[:, :, 0:1], 0.0))
                link.sig(V.memset(cur[:, :], 0.0))
                link.step(V.memset(gate_pad, 0.0))
                v.wait_ge(y_ready, Y0)

                def moments(q):
                    v.wait_ge(x_loaded[q], 16)
                    for i in range(QT * q, QT * q + QT):
                        V.bn_stats(stats[:, i, :], x_in[:, i, :]).then_inc(stats_ready, 1)
                    v.wait_ge(stats_ready, QT * (q + 1))
                    for i in range(QT * q, QT * q + QT):
                        link.sig(V.bn_aggr(mv[:, i, :], stats[:, i, :]))
                    v.wait_ge(route, link.n)
                    V.tensor_scalar(small[:, 0, QT * q:QT * q + QT], mv[:, QT * q:QT * q + QT, 1], EPS_LN, None,
                                    ALU.add).then_inc(var_ready, 1)

                def norm(q):
                    v.wait_ge(pow_ready, power(q, 0))
                    t = slice(QT * q, QT * q + QT)
                    link.step(V.tensor_tensor(small[:, 4, t], mv[:, t, 1], small[:, 1, t], ALU.mult))
                    link.step(V.tensor_tensor(small[:, 5, t], small[:, 4, t], small[:, 1, t], ALU.mult))
                    V.tensor_scalar(small[:, 2, t], small[:, 5, t], EPS_RMS, None, ALU.add).then_inc(var_ready, 1)
                    for i in range(QT * q, QT * q + QT):
                        V.tensor_scalar(xa[:, i, 0:D], x_in[:, i, :], mv[:, i, 0:1], small[:, 1, i:i + 1],
                                        ALU.subtract, ALU.mult).then_inc(xn_ready, 1)

                def copy_xnT(s):
                    v.wait_ge(xnT_made, s + 1)
                    V.tensor_copy(xnT[:, s, :], pG[s % 2][:, :]).then_inc(xnT_ready, 1)

                moments(0)
                moments(1)
                norm(0)
                moments(2)
                norm(1)
                v.wait_ge(first_loaded, 16 * NFIRST)
                for s in range(NSEG):
                    ins = V.tensor_copy(gate_pad[:, s, s * E:(s + 1) * E], gate[:, :])
                ins.then_inc(gate_ready, 1)
                moments(3)
                norm(2)
                copy_xnT(0)
                copy_xnT(1)
                norm(3)
                mixes(0, (MIX_R, MIX_K, MIX_V, MIX_G, MIX_W))
                copy_xnT(2)
                copy_xnT(3)
                weigh_own(0)
                copy_xnT(4)
                copy_xnT(5)
                own(0)
                copy_xnT(6)
                copy_xnT(7)
                v.wait_ge(hT_ready, NSEG)
                hb = hT[:, :, :].rearrange("p (b c) t -> p b c t", b=B)
                for b in range(B):
                    ins = V.tensor_copy(hb[:, b, 1:SPB, 0], hb[:, b, 0:SPB - 1, SEG])
                ins.then_inc(edges_ready, 1)
                v.wait_ge(exp_ready, 1)
                link.step(V.tensor_scalar(junk, gt, 1.0, None, ALU.add))
                link.step(V.reciprocal(score, junk))
                mixes(1, (MIX_R, MIX_K, MIX_V, MIX_G, MIX_W))
                v.wait_ge(consts_loaded, 16 * (len(const_loads) - NFIRST))
                pass_(0, searching=True, finish=False)
                with v.Fori(1, 3) as p:
                    pass_(p, searching=True)
                pass_(LIST_PASS, listing=True)
                for t in sum_set:
                    v.wait_ge(t, 16 * NSEG // 2)
                with v.Fori(4, 6) as p:
                    pass_(p, experts=True)
                pass_(6, experts=True, mixing=False)
                last_pass(LAST)

            @block.scalar
            def _(act):
                A = nc.scalar

                def take(name, c, out, func, **kw):
                    after(act, made[name], c + 1)
                    return A.activation(out, pR[BANK[name]][0:out.shape[0], :], func, **kw).then_inc(taken[name], 1)

                def step_up(c):
                    after(act, rs_ready, DK * c)
                    after(act, taken["R"], c + 1)
                    A.activation(r_cur, r_next, ACT.Copy).then_inc(rcur_ready, 1)
                    after(act, dec_made, c * 2 + 2)
                    A.activation(dec, ew, ACT.Copy).then_inc(dec_ready, 1)

                def squares(c):
                    after(act, made["O"], c + 1)
                    A.activation(og, pO[:, :], ACT.Square).then_inc(sq_ready, 1)

                def rstd(c):
                    take("VAR", c, og, ACT.Ln, bias=vec[:, EPSG:EPSG + 1])
                    after(act, taken["VAR"], c + 1)
                    A.activation(og, og, ACT.Exp, scale=-0.5).then_inc(rstd_ready, 1)

                def take_r(c):
                    after(act, ruk_ready, c)
                    after(act, rcur_ready, c)
                    take("R", c, r_next, ACT.Copy)

                def take_kv(c):
                    after(act, kv_ready, DK * c)
                    take("K", c, k_sb, ACT.Copy)
                    after(act, taken["C"], c)
                    after(act, v_stored, 16 * c)
                    take("V", c, v_sb, ACT.Copy)

                def scale_norm(c):
                    after(act, taken["O"], c + 1)
                    A.activation(og, og, ACT.Identity, scale=vec[:, GNW:GNW + 1],
                                 bias=vec[:, GNB:GNB + 1]).then_inc(gn_ready, 1)

                def tanh(c):
                    after(act, dec_ready, c)
                    take("A", c, ew[0:LORA, :], ACT.Tanh)

                def decay(c):
                    after(act, made["B"], c + 1)
                    A.activation(ew, pR[BANK["B"]][:, :], ACT.Exp, bias=vec[:, W0:W0 + 1]).then_inc(dec_made, 1)
                    after(act, dec_made, c * 2 + 1)
                    A.activation(ew, ew, ACT.Exp, scale=-1.0).then_inc(dec_made, 1)

                def gate_next(c):
                    if not (isinstance(c, int) and c == 0):
                        after(act, og_ready, c - 1)
                        after(act, taken["G"], c)
                        A.activation(g_cur, g_next, ACT.Copy).then_inc(gcur_ready, 1)
                        after(act, gcur_ready, c)
                    take("G", c, g_next, ACT.Silu)

                def h2_out(c):
                    take("H2", c, h2T[:, :], ACT.Copy, scale=vec[:, LN2:LN2 + 1])

                def gelu(c, f):
                    after(act, made["F"], c * NF + f + 1)
                    A.activation(gl[:, f, :], pR[F_BANK[f]][:, :], ACT.Gelu).then_inc(taken["F"], 1)

                def shared_step(p, half, f):
                    n = p * 4 + half * 2 + f
                    after(act, pY_made, p * 2 + half)
                    after(act, sh_made, n + 1)
                    A.activation(shs[:, f, :], pG[f][:, :], ACT.Silu).then_inc(shs_ready, 1)
                    A.activation(shu[:, f, :], pU[0][:, :], ACT.Copy).then_inc(shu_ready, 1)

                def shared_out(c, n):
                    after(act, pY_made, n)
                    A.activation(cols(xnT[:, :, :], c), pY[:, :], ACT.Copy).then_inc(pY_taken, 1)

                def bias_out(c):
                    after(act, pY_made, 8 + c)
                    if c >= 2:
                        after(act, sum_set[c % 2], 16 * (c // 2))
                    A.activation(y[:, c % 2, :, :], pY[:, :].rearrange("p (b c) -> p b c", b=NB),
                                 ACT.Copy).then_inc(pY_taken, 1)

                def silu_step(e, f):
                    after(act, gu_made, e * NF + f + 1)
                    A.activation(sg[:, f % 2, :], pG[f % 2][:, :], ACT.Silu,
                                 bias=ex_bias[:, 0, bass.ds(e * NF + f, 1)]).then_inc(sg_ready, 1)

                def x_out(e, s):
                    after(act, xT_made, e + 1)
                    A.activation(xinT[:, s % 2, :], pY[:, :], ACT.Copy).then_inc(xT_ready, 1)

                def first_row(p, finish, listing=False):
                    step_up(p)
                    if finish:
                        squares(p - 1)
                        rstd(p - 1)
                    take_r(p + 1)
                    if finish:
                        scale_norm(p - 1)
                    take_kv(p + 1)
                    shared_step(p, 0, 0)
                    tanh(p + 1)
                    shared_step(p, 0, 1)
                    decay(p + 1)
                    gate_next(p + 1)
                    shared_out(p * 2, p * 2 + 1)
                    if listing:
                        bias_out(0)
                        bias_out(1)
                    shared_step(p, 1, 0)
                    if finish:
                        h2_out(p - 1)
                    if listing:
                        bias_out(2)
                        bias_out(3)
                    shared_step(p, 1, 1)
                    if listing:
                        bias_out(4)
                        bias_out(5)
                    if finish:
                        for f in range(NF):
                            gelu(p - 1, f)
                    if listing:
                        bias_out(6)
                        bias_out(7)
                    shared_out(p * 2 + 1, 16 if listing else p * 2 + 2)

                def second_row(p):
                    for i in range(DK):
                        e = p * EP - 4 * EP + i // 2
                        f = 2 * (i % 2)
                        if i == 0:
                            step_up(p)
                            squares(p - 1)
                        silu_step(e, f)
                        silu_step(e, f + 1)
                        if i % 2 == 1:
                            x_out(e + 1, i // 2 + 1)
                        if i == 0:
                            rstd(p - 1)
                            take_r(p + 1)
                            scale_norm(p - 1)
                        if i == 1:
                            take_kv(p + 1)
                        if i == 2:
                            tanh(p + 1)
                        if i == 3:
                            decay(p + 1)
                        if i == 4:
                            gate_next(p + 1)
                        if i == 5:
                            h2_out(p - 1)
                        if i == 7:
                            for k in range(NF):
                                gelu(p - 1, k)

                def last_row(p):
                    step_up(p)
                    for i in range(DK):
                        e = p * EP - 4 * EP + i // 2
                        f = 2 * (i % 2)
                        c = p - 1 + i // 4
                        if i % 4 == 0:
                            squares(c)
                        silu_step(e, f)
                        silu_step(e, f + 1)
                        if i % 2 == 1 and i < 7:
                            x_out(e + 1, i // 2 + 1)
                        if i % 4 == 0:
                            rstd(c)
                            scale_norm(c)
                        if i == 2:
                            after(act, og_ready, c + 1)
                            after(act, taken["G"], NSEG)
                            A.activation(g_cur, g_next, ACT.Copy).then_inc(gcur_ready, 1)
                        if i % 4 == 3:
                            h2_out(c)
                            for k in range(NF):
                                gelu(c, k)

                act.wait_ge(first_loaded, 16 * NFIRST)
                for _ in range(F0_):
                    A.activation(g_cur[:, 0:1], vec[:, 0:1], ACT.Copy).then_inc(taken["F"], 1)
                def first_norm(q):
                    act.wait_ge(pow_ready, power(q, 1))
                    act.wait_ge(xn_ready, QT * (q + 1))
                    for i in range(QT * q, QT * q + QT):
                        A.activation(hrow[:, i, :], xa[:, i, 0:D], ACT.Copy,
                                     scale=small[:, 3, i:i + 1]).then_inc(hrow_ready, 1)
                    for s in (2 * q, 2 * q + 1):
                        act.wait_ge(hT_made, s + 1)
                        A.activation(hT[:, s, 1:SEG + 1], pU[s % 2][:, :], ACT.Copy,
                                     scale=vec[:, LN1:LN1 + 1]).then_inc(hT_ready, 1)

                first_norm(0)
                first_norm(1)
                take_r(0)
                take_kv(0)
                tanh(0)
                first_norm(2)
                decay(0)
                first_norm(3)
                act.wait_ge(logits_ready, 1)
                A.activation(gt, pY[:, :], ACT.Exp, scale=-1.0).then_inc(exp_ready, 1)
                gate_next(0)
                act.wait_ge(consts_loaded, 16 * (len(const_loads) - NFIRST))
                first_row(0, False)
                with act.Fori(1, 3) as p:
                    first_row(p, True)
                first_row(LIST_PASS, True, True)
                x_out(0, 0)
                with act.Fori(4, 7) as p:
                    second_row(p)
                last_row(LAST)

            @block.tensor
            def _(pe):
                X = nc.tensor

                def proj(name, m, c, *before):
                    for s, n in before:
                        after(pe, s, n)
                    after(pe, mix_ready, 5 * c + m + 1)
                    w = w_a[:, :] if name == "A" else w_rkvg[:, m, :]
                    o = pR[BANK[name]]
                    X.matmul(o[0:LORA, :] if name == "A" else o[:, :], w, mix[:, m, :], start=True,
                             stop=True).then_inc(made[name], 1)

                def lora_out(c):
                    after(pe, taken["V"], c + 1)
                    after(pe, taken["A"], c + 1)
                    X.matmul(pR[BANK["B"]][:, :], w_b[:, :], ew[0:LORA, :], start=True, stop=True
                             ).then_inc(made["B"], 1)

                def own(c):
                    after(pe, dec_made, c * 2 + 1)
                    after(pe, ruk_ready, c + 1)
                    X.matmul(pR[BANK["C"]][:, :], headones[:, :], ruk, start=True, stop=True).then_inc(made["C"], 1)

                def open_o(c):
                    after(pe, taken["O"], c)
                    after(pe, taken["C"], c + 1)
                    X.matmul(pO[:, :], center[:, :], cv, start=True, stop=False)

                def add_o(c, i):
                    after(pe, rs_ready, DK * c + i + 1)
                    ins = X.matmul(pO[:, :], selc[:, i, :], rs[:, i % 2, :], start=False, stop=(i == DK - 1))
                    ins.then_inc(made["O"] if i == DK - 1 else rs_used, 1)

                def var(c):
                    after(pe, taken["FO"], c + FO0)
                    if not (isinstance(c, int) and c == LAST):
                        after(pe, taken["G"], c + 2)
                    after(pe, sq_ready, c + 1)
                    X.matmul(pR[BANK["VAR"]][:, :], headmean[:, :], og, start=True, stop=True).then_inc(made["VAR"], 1)

                def w_out(c, *before):
                    for s, n in before:
                        after(pe, s, n)
                    after(pe, og_ready, c + 1)
                    for b in range(NB):
                        ins = X.matmul(pR[BANK["WO"]][:, b * P:(b + 1) * P], og[:, b * P:(b + 1) * P], w_o[:, :],
                                       start=True, stop=True)
                    ins.then_inc(made["WO"], 1)

                def turn_h2(c, *before):
                    for s, n in before:
                        after(pe, s, n)
                    after(pe, h2_ready, c + 1)
                    for b in range(NB):
                        ins = X.transpose(pR[BANK["H2"]][:, b * P:(b + 1) * P], h2[:, b, :], ident[:, :])
                    ins.then_inc(made["H2"], 1)

                def ff1(c, f, *before):
                    for s, n in before:
                        after(pe, s, n)
                    if f == 0:
                        after(pe, taken["H2"], c + 1)
                    if f >= 2:
                        after(pe, taken["F"], c * NF + f - 1 + F0_)
                    X.matmul(pR[F_BANK[f]][:, :], w_f1[:, f * P:(f + 1) * P], h2T[:, :], start=True, stop=True
                             ).then_inc(made["F"], 1)

                def ff2(c):
                    after(pe, taken["F"], c * NF + NF + F0_)
                    for b in range(NB):
                        for f in range(NF):
                            ins = X.matmul(pR[BANK["FO"]][:, b * P:(b + 1) * P], gl[:, f, b * P:(b + 1) * P],
                                           w_f2[:, f, :], start=(f == 0), stop=(f == NF - 1))
                    ins.then_inc(made["FO"], 1)

                def shared_up(p, half, f):
                    n = p * 4 + half * 2 + f
                    after(pe, shs_ready, n - 1)
                    after(pe, shu_ready, n)
                    if isinstance(p, int) and p == LIST_PASS and half:
                        pe.wait_ge(slotT_used, 2)
                    rhs = cols(xnT[:, :, :], p * 2 + half)
                    X.matmul(pG[f][:, :], sh_gu[:, 0, f * P:(f + 1) * P], rhs, start=True, stop=True)
                    X.matmul(pU[0][:, :], sh_gu[:, 1, f * P:(f + 1) * P], rhs, start=True, stop=True
                             ).then_inc(sh_made, 1)

                def shared_down(c, n):
                    after(pe, shh_ready, c * 2 + 2)
                    after(pe, pY_taken, n - 1)
                    for b in range(NB):
                        for f in range(2):
                            ins = X.matmul(pY[:, b * P:(b + 1) * P], shs[:, f, b * P:(b + 1) * P], sh_dn[:, f, :],
                                           start=(f == 0), stop=(f == 1))
                    ins.then_inc(pY_made, 1)

                def bias_sum(c):
                    pe.wait_ge(selscore_ready, 1)
                    pe.wait_ge(pY_taken, 7 + c)
                    for b in range(NB):
                        ins = X.matmul(pY[:, b * P:(b + 1) * P], selscore[:, b * P:(b + 1) * P], down_b[:, c, :],
                                       start=True, stop=True)
                    ins.then_inc(pY_made, 1)

                def total(j):
                    after(pe, count_ready, j + 1)
                    X.matmul(pU[1][:, 0:1], segones[:, :], cnt[:, 0:1], start=True, stop=True).then_inc(total_ready, 1)

                def sums():
                    pe.wait_ge(count_ready, NBITS + 1)
                    X.matmul(pU[1][:, 0:2], segones[:, :], cnt[:, 0:2], start=True, stop=True)
                    X.matmul(pU[1][:, 2:4], seglow[:, :], cnt[:, 0:2], start=True, stop=True).then_inc(total_ready, 1)

                def offsets():
                    pe.wait_ge(count_ready, NBITS + 2)
                    X.matmul(pU[1][:, 4:5], seglow[:, :], cnt[:, 2:3], start=True, stop=True).then_inc(total_ready, 1)

                def turn_slots():
                    pe.wait_ge(slot_ready, 1)
                    pe.wait_ge(shs_ready, 14)
                    for b in range(NB):
                        X.transpose(pG[0][:, b * P:(b + 1) * P], gt[:, b * P:(b + 1) * P], ident[:, :])
                        ins = X.transpose(pG[1][:, b * P:(b + 1) * P], score[:, b * P:(b + 1) * P], ident[:, :])
                    ins.then_inc(slotT_ready, 1)

                def list_half(half):
                    pe.wait_ge(onehot_ready, half + 1)
                    for t in range(NT // 2):
                        for g in range(E // 4):
                            c = t * E + 4 * g
                            ins = X.matmul(pU[1][:, 64 * g:64 * g + 64],
                                           one_a[:, c:c + 4, :].rearrange("p e s -> p (e s)"),
                                           one_b[:, :, c:c + 4].rearrange("p s e -> p e s"),
                                           start=(half == 0 and t == 0 and g == 0),
                                           stop=(half == 1 and t == NT // 2 - 1), skip_group_check=True)
                    ins.then_inc(list_ready if half else onehot_used, 1)

                def spread_list():
                    pe.wait_ge(list_used, 1)
                    pe.wait_ge(shs_ready, 16)
                    pe.wait_ge(shu_ready, 16)
                    for e4 in range(4):
                        rr = slice(32 * e4, 32 * e4 + 32)
                        for c in range(4):
                            ins = X.matmul((pG + pU)[e4][32 * c:32 * c + 32, 0:16], ident[rr, rr],
                                           list_ab[rr, :, :].rearrange("p g (q c) -> p c g q", c=4)[:, c],
                                           start=True, stop=True, tile_position=(32 * e4, 32 * c))
                    ins.then_inc(idx_made, 1)

                def turn_x(e, s):
                    after(pe, gathered[s % 2], e_half(e, s) * 16 * NB + 16 * NB)
                    after(pe, y_ready, e - 1 + Y0)
                    for b in range(NB):
                        ins = X.transpose(pY[:, b * P:(b + 1) * P], xg[:, s % 2, b, 0:D], ident[:, :])
                    ins.then_inc(xT_made, 1)

                def e_half(e, s):
                    return e // 2 if isinstance(e, int) else eh[0] + s // 2

                eh = [0]

                def expert_step(e, s, f):
                    if f == 0:
                        after(pe, xT_ready, e + 1)
                        after(pe, w_loaded[s % 2], e_half(e, s) * 32 + 32)
                    after(pe, hid_ready, e * NF + f - 1 + HID0)
                    rhs = xinT[:, s % 2, :]
                    X.matmul(pG[f % 2][:, :], wx[:, s % 2, 0, f * P:(f + 1) * P], rhs, start=True, stop=True)
                    X.matmul(pU[f % 2][:, :], wx[:, s % 2, 1, f * P:(f + 1) * P], rhs, start=True, stop=True
                             ).then_inc(gu_made, 1)

                def expert_down(e, s, more):
                    after(pe, hid_ready, e * NF + NF + HID0)
                    after(pe, xT_ready, e + 2 if more else e + 1)
                    after(pe, y_ready, e + Y0)
                    for b in range(NB):
                        for f in range(NF):
                            ins = X.matmul(pY[:, b * P:(b + 1) * P], hid[:, f, b * P:(b + 1) * P],
                                           wx[:, s % 2, 2, f * P:(f + 1) * P], start=(f == 0), stop=(f == NF - 1))
                    ins.then_inc(y_made, 1)

                def pass_(p, searching=False, listing=False, experts=False, finish=True):
                    if experts and not isinstance(p, int):
                        eh[0] = p * 2 - 8
                    c = p + 1
                    for i in range(DK):
                        e = p * EP - 4 * EP + i // 2
                        s, f = i // 2, 2 * (i % 2)
                        if experts:
                            expert_step(e, s, f)
                            expert_step(e, s, f + 1)
                        if i == 0:
                            if finish:
                                var(p - 1)
                            proj("R", MIX_R, c, (taken["F"], (p - 2) * NF + NF + F0_), (taken["C"], c))
                        if i == 1:
                            proj("K", MIX_K, c, *([(taken["VAR"], p)] if finish else [(taken["G"], c)]))
                            proj("V", MIX_V, c, (taken["R"], c + 1))
                        if experts and i % 2 == 1:
                            turn_x(e + 1, s + 1)
                        if i == 1:
                            if not experts:
                                shared_up(p, 0, 0)
                            if searching:
                                total(p * PER)
                            open_o(p)
                            add_o(p, 0)
                        if i == 2:
                            proj("A", MIX_W, c, (taken["K"], c + 1))
                            if not experts:
                                shared_up(p, 0, 1)
                        if i == 3:
                            lora_out(c)
                            if finish:
                                w_out(p - 1, (taken["A"], c + 1))
                        if i == 4:
                            own(c)
                            proj("G", MIX_G, c, (taken["WO"], p) if finish else (taken["A"], c + 1))
                            if not experts:
                                shared_down(p * 2, p * 2 + 1)
                            if listing:
                                bias_sum(0)
                                bias_sum(1)
                        if i == 5:
                            if not experts:
                                shared_up(p, 1, 0)
                            if finish:
                                turn_h2(p - 1, (taken["C"], c + 1))
                            if listing:
                                bias_sum(2)
                                bias_sum(3)
                        if i == 6:
                            if not experts:
                                shared_up(p, 1, 1)
                            if listing:
                                bias_sum(4)
                                bias_sum(5)
                            if finish:
                                ff1(p - 1, 0, (taken["G"], c + 1))
                                ff1(p - 1, 1)
                        if searching and 2 <= i <= PER // 2:
                            total(p * PER + 2 * i - 2)
                        if i:
                            add_o(p, i)
                        if experts and i % 2 == 1:
                            expert_down(e, s, True)
                        if listing:
                            (sums, offsets, turn_slots, lambda: None, lambda: None,
                             lambda: list_half(0), lambda: list_half(1), spread_list)[i]()
                        if i == 7:
                            if finish:
                                ff1(p - 1, 2)
                                ff1(p - 1, 3)
                            if listing:
                                bias_sum(6)
                                bias_sum(7)
                            if finish:
                                ff2(p - 1)
                            if not experts:
                                shared_down(p * 2 + 1, 16 if listing else p * 2 + 2)
                        if searching and 1 <= i <= PER // 2:
                            total(p * PER + 2 * i - 1)

                def last_pass(p):
                    for i in range(DK):
                        e = p * EP - 4 * EP + i // 2
                        s, f = i // 2, 2 * (i % 2)
                        c = p - 1 + i // 4
                        expert_step(e, s, f)
                        expert_step(e, s, f + 1)
                        if i % 4 == 0:
                            var(c)
                        if i % 2 == 1 and i < 7:
                            turn_x(e + 1, s + 1)
                        if i == 1:
                            open_o(p)
                        if i % 4 == 3:
                            turn_h2(c, (taken["F"], c * NF + F0_))
                        for k in ((), (0, 1, 2, 3), (4, 5), (6, 7))[i] if i < 4 else ():
                            add_o(p, k)
                        if i % 4 == 1:
                            w_out(c, (taken["VAR"], c + 1))
                        if i % 4 == 3:
                            ff1(c, 0, (taken["WO"], c + 1))
                            ff1(c, 1)
                        if i % 2 == 1:
                            expert_down(e, s, i < 7)
                        if i % 4 == 3:
                            ff1(c, 2)
                            ff1(c, 3)
                            ff2(c)

                def turn_rows(s):
                    pe.wait_ge(xn_ready, NB * (s + 1))
                    if s >= 2:
                        pe.wait_ge(xnT_ready, s - 1)
                    for b in range(NB):
                        ins = X.transpose(pG[s % 2][:, b * P:(b + 1) * P], xa[:, NB * s + b, 0:D], ident[:, :])
                    ins.then_inc(xnT_made, 1)
                    pe.wait_ge(hrow_ready, NB * (s + 1))
                    if s >= 2:
                        pe.wait_ge(hT_ready, s - 1)
                    for b in range(NB):
                        ins = X.transpose(pU[s % 2][:, b * P:(b + 1) * P], hrow[:, NB * s + b, :], ident[:, :])
                    ins.then_inc(hT_made, 1)

                pe.wait_ge(first_loaded, 16 * NFIRST)
                X.matmul(pY[0:2, 0:2], ident[:, 0:2], ident[:, 0:2], start=True, stop=True).then_inc(y_made, YM0)
                for t in range(4):
                    turn_rows(t)
                pe.wait_ge(consts_loaded, 16 * (len(const_loads) - NFIRST))
                proj("R", MIX_R, 0)
                proj("K", MIX_K, 0)
                proj("V", MIX_V, 0, (taken["R"], 1))
                proj("A", MIX_W, 0, (taken["K"], 1))
                turn_rows(4)
                turn_rows(5)
                lora_out(0)
                own(0)
                proj("G", MIX_G, 0, (taken["A"], 1))
                turn_rows(6)
                turn_rows(7)
                pe.wait_ge(gate_ready, 1)
                for t in range(NSEG):
                    pe.wait_ge(xnT_ready, t + 1)
                    ins = X.matmul(pY[:, :], gate_pad[:, t, :], xnT[:, t, :], start=(t == 0), stop=(t == NSEG - 1))
                ins.then_inc(logits_ready, 1)
                pe.wait_ge(hT_ready, NSEG)
                pe.wait_ge(exp_ready, 1)
                pe.wait_ge(bias_loaded, 16 * NSEG)
                pass_(0, searching=True, finish=False)
                with pe.Fori(1, 3) as p:
                    pass_(p, searching=True)
                pass_(LIST_PASS, listing=True)
                pe.wait_ge(pY_taken, 16)
                turn_x(0, 0)
                with pe.Fori(4, 7) as p:
                    pass_(p, experts=True)
                last_pass(LAST)

        fin_loaded = [sem(f"fin_loaded{q}") for q in range(4)]
        sum_ready = sem("sum_ready")
        act_ready = sem("act_ready")
        prod_ready = sem("prod_ready")
        fin_ready = sem("fin_ready")
        out_stored = sem("out_stored")
        share = xnT[:, :, :].rearrange("p s (b c) -> p s b c", b=NB)
        s_all = hT[:, :, 0:SEG].rearrange("p s (b c) -> p s b c", b=NB)
        x_all = xa[:, :, 0:D].rearrange("p (s b) c -> p s b c", b=NB)
        m_all = moe.rearrange("p (s b) c -> p s b c", b=NB)
        with nc.Block() as block:
            @block.sync
            def _(sp):
                view = lambda t: t.rearrange("(q i p) c -> q p i c", p=P, q=4)
                for q in range(4):
                    sp.dma_start(moe[:, QT * q:QT * q + QT, :], view(moe_sum[:, :])[q]).then_inc(fin_loaded[q], 16)
                for q in range(4):
                    sp.wait_ge(fin_ready, 2 * q + 2)
                    sp.dma_start(view(out)[q], moe[:, QT * q:QT * q + QT, :]).then_inc(out_stored, 16)
                sp.wait_ge(out_stored, 64)

            @block.vector
            def _(v):
                for c in range(NSEG + 1):
                    if c < NSEG:
                        v.wait_ge(fin_loaded[c // 2], 16)
                        nc.vector.tensor_tensor(m_all[:, c], m_all[:, c], share[:, c], ALU.add).then_inc(sum_ready, 1)
                    if c:
                        v.wait_ge(act_ready, c)
                        nc.vector.tensor_tensor(s_all[:, c - 1], s_all[:, c - 1], share[:, c - 1],
                                                ALU.mult).then_inc(prod_ready, 1)
                        v.wait_ge(prod_ready, c)
                        nc.vector.tensor_tensor(m_all[:, c - 1], x_all[:, c - 1], s_all[:, c - 1],
                                                ALU.add).then_inc(fin_ready, 1)

            @block.scalar
            def _(act):
                for c in range(NSEG):
                    act.wait_ge(sum_ready, c + 1)
                    nc.scalar.activation(share[:, c], m_all[:, c], ACT.Silu).then_inc(act_ready, 1)


def shape_constants():
    f = np.float32
    k = np.arange(P)
    same_head = (k[:, None] // DK == k[None, :] // DK)
    c = {"ident": np.eye(P), "headones": same_head, "headmean": same_head / DK,
         "center": np.eye(P) - same_head / DK}
    c["selc"] = same_head[:, None, :] * ((k[None, None, :] % DK == np.arange(DK)[None, :, None]) - 1.0 / DK)
    same_expert = (k[:, None] % E == k[None, :] % E)
    c["segones"] = same_expert
    c["seglow"] = same_expert & (k[:, None] // E < k[None, :] // E)
    c = {n: np.ascontiguousarray(a, f) for n, a in c.items()}
    c["bits"] = np.ascontiguousarray(np.broadcast_to(1 << np.arange(NBITS - 1, -1, -1), (P, NBITS)), np.int32)
    c["iota_a"] = np.ascontiguousarray(np.broadcast_to(np.arange(SA), (P, SA)), np.float16)
    blk, seg = np.meshgrid(np.arange(NB), np.arange(NSEG), indexing="ij")
    base = np.repeat((seg * SEG + blk * P).ravel(), E)
    c["tokval"] = (base[None, :] + k[:, None] - TOK // 2).astype(np.float16)
    return c


def kernel(**inputs):
    import concourse.bacc as bacc
    from concourse.bass_utils import run_bass_kernel_spmd

    a = {n: np.asarray(x) for n, x in inputs.items()}
    L = {n[len("L0_attn_"):]: x for n, x in a.items() if n.startswith("L0_attn_")}
    M = {n[len("L0_ffn_"):]: x for n, x in a.items() if n.startswith("L0_ffn_")}
    f = np.float32
    eps = np.full((P,), EPS_GN, f)
    arrays = shape_constants()
    arrays["x"] = L["x"].reshape(TOK, D)
    arrays["vec"] = np.stack([L["ln1_w"], L["mu_r"], L["mu_k"], L["mu_v"], L["mu_w"], L["mu_g"], L["w0"],
                              L["u"].reshape(P), L["gn_w"].reshape(P), L["gn_b"].reshape(P), L["ln2_w"], eps], 1)
    arrays["w_rkvg"] = np.stack([L["Wr"], L["Wk"], L["Wv"], L["Wg"]], 1)
    arrays["w_a"], arrays["w_b"], arrays["w_o"] = L["wA"], L["wB"], L["Wo"]
    arrays["w_f1"] = L["ffn_w1"]
    arrays["w_f2"] = L["ffn_w2"].reshape(NF, P, D).transpose(1, 0, 2)
    arrays["gate"] = M["gate_w"].T
    arrays["sh_gu"] = np.stack([M["sh_gate_w"].T, M["sh_up_w"].T], 1)
    arrays["sh_dn"] = M["sh_down_w"].T.reshape(2, P, D).transpose(1, 0, 2)
    arrays["down_b"] = M["down_b"]
    arrays["ex_bias"] = np.stack([M["gb"].reshape(E * NF, P).T, M["up_b"].reshape(E * NF, P).T], 1)
    arrays["ex_gu"] = np.stack([M["gw"].transpose(0, 2, 1), M["up_w"].transpose(0, 2, 1)], 2)
    arrays["ex_dn"] = M["down_w"].transpose(0, 2, 1).reshape(E, NF, P, D).transpose(0, 2, 1, 3).reshape(E, P, FF)
    arrays = {n: np.ascontiguousarray(x) for n, x in arrays.items()}

    nc = bacc.Bacc("TRN2", target_bir_lowering=False, num_devices=1)
    d = {n: nc.dram_tensor("in_" + n, x.shape, mybir.dt.from_np(x.dtype), kind="ExternalInput").ap()
         for n, x in arrays.items()}
    out = nc.dram_tensor("out", (TOK, D), F32, kind="ExternalOutput").ap()
    build(nc, d, out)
    r = run_bass_kernel_spmd(nc, [{"in_" + n: x for n, x in arrays.items()}], core_ids=[0])
    return r.results[0]["out"].reshape(B, T, D)
```

```python
from contextlib import ExitStack

import numpy as np

import concourse.bass as bass
from concourse import mybir

ALU = mybir.AluOpType
ACT = mybir.ActivationFunctionType
F32 = mybir.dt.float32
F16 = mybir.dt.float16
I32 = mybir.dt.int32

P = 128
B, T, D = 2, 2048, 128
H, DK = 16, 8
LORA = 64
FF = 512
NF = FF // P
E, TOPK = 16, 2
SH = 256
TOK = B * T
CAP = TOK // E * TOPK
SEG = 512
NSEG = TOK // SEG
SPB = T // SEG
NB = SEG // P
NT = TOK // P
ROW = D + E
SHIGH, SLOW = 32, 16
NBITS = 30
EPS_LN, EPS_RMS, EPS_GN = 1e-5, 1e-6, 1e-5
LN1, MU_R, MU_K, MU_V, MU_W, MU_G, W0, U, GNW, GNB, LN2, EPSG, NVEC = range(13)
MIX_R, MIX_K, MIX_V, MIX_G, MIX_W = range(5)
MUS = (MU_R, MU_K, MU_V, MU_G, MU_W)


class Count:

    def __init__(self, sem, engine):
        self.sem, self.engine, self.n = sem, engine, 0

    def sig(self, ins):
        ins.then_inc(self.sem, 1)
        self.n += 1

    def step(self, ins):
        self.sig(ins)
        self.engine.wait_ge(self.sem, self.n)


def build(nc, d, out):
    ctx = ExitStack()
    with ctx:
        def sb(name, shape, dt=F32):
            return ctx.enter_context(nc.sbuf_tensor(name, shape, dt))

        def ps(name, shape, dt=F32):
            return ctx.enter_context(nc.psum_tensor(name, shape, dt))

        def sem(name):
            return ctx.enter_context(nc.semaphore(name))

        rows = nc.dram_tensor("row_table", [TOK, ROW], F32)
        moe_sum = nc.dram_tensor("moe_sum", [TOK, D], F32)
        v_dram = nc.dram_tensor("v_dram", [P, SEG], F32)

        ident = sb("ident", [P, P])
        selc = sb("selc", [P, DK, P])
        center = sb("center", [P, P])
        headmean = sb("headmean", [P, P])
        headones = sb("headones", [P, P])
        segones = sb("segones", [P, P])
        seglow = sb("seglow", [P, P])
        bits = sb("bits", [P, NBITS], I32)
        tokval = sb("tokval", [P, NB * P], F16)
        iota = sb("iota", [P, SHIGH * 4], F16)
        own4 = sb("own4", [P, 4])
        vec = sb("vec", [P, NVEC])
        w_rkvg = sb("w_rkvg", [P, 4, P])
        w_o = sb("w_o", [P, P])
        w_a = sb("w_a", [P, LORA])
        w_b = sb("w_b", [LORA, P])
        w_f1 = sb("w_f1", [P, FF])
        w_f2 = sb("w_f2", [P, NF, P])
        gate = sb("gate", [P, E])
        sh_gu = sb("sh_gu", [P, 2, SH])
        sh_dn = sb("sh_dn", [P, 2, P])
        ex_bias = sb("ex_bias", [P, 2, E * NF])

        xa = sb("xa", [P, NT, ROW])
        xnT = sb("xnT", [P, NSEG, SEG])
        hT = sb("hT", [P, NSEG, SEG + 1])
        mv = sb("mv", [P, NT, 2])
        small = sb("small", [P, 6, NT])
        minus_half = sb("minus_half", [P, NT])
        cur = sb("cur", [P, 1])
        cand = sb("cand", [P, 1])
        kept = sb("kept", [P, 1])
        cnt = sb("cnt", [P, 4])
        lim = sb("lim", [P, 2])
        idx = sb("idx", [P, E * NB], I32)
        idx_e = sb("idx_e", [P, 4, NB], I32)
        ms = sb("ms", [P, 3, NB])

        def region(name, size):
            t = sb(name, [P, size])
            at = [0]

            def carve(*shape):
                n = int(np.prod(shape))
                ap = t[:, at[0]:at[0] + n]
                at[0] += n
                assert at[0] <= size, (name, at[0])
                return ap.rearrange("p (a b) -> p a b", a=shape[0]) if len(shape) == 2 else ap

            def restart():
                at[0] = 0
            return carve, restart

        carve, restart = region("state", 2 * DK * SEG + DK)
        x_in = carve(NT, P)
        hrow = carve(NT, P)
        restart()
        vb = carve(DK, SEG)
        kvS = carve(DK, SEG + 1)
        moe = vb.rearrange("p v t -> p (v t)").rearrange("p (i c) -> p i c", c=P)

        mix = sb("mix", [P, 5, SEG])
        rs = sb("rs", [P, 2, SEG])
        r_next, r_cur, k_sb, v_sb, g_next, g_cur, ew, dec, ruk, cv, og = (
            sb(n, [P, SEG])[:, :] for n in
            ("r_next", "r_cur", "k_sb", "v_sb", "g_next", "g_cur", "ew", "dec", "ruk", "cv", "og"))
        x2 = sb("x2", [P, NB, P])
        h2 = sb("h2", [P, NB, P])
        h2T = sb("h2T", [P, SEG])
        gl = sb("gl", [P, NF, SEG])

        HT = NB * P // 2
        carve, restart = region("second", 9280)
        shs = carve(2, SEG)
        shu = carve(2, SEG)
        down_b = carve(NSEG, P)
        one_a = carve(SHIGH * HT // 2).bitcast(F16).rearrange("p (g s e) -> p g s e", s=SHIGH, e=4)
        one_b = carve(SLOW * HT // 2).bitcast(F16).rearrange("p (g s e) -> p g s e", s=SLOW, e=4)
        list_ab = carve(E // 4, SLOW)
        stats = shu[:, :, :].rearrange("p a b -> p (a b)")[:, 0:NT * 6].rearrange("p (i c) -> p i c", c=6)
        gate_pad = one_a.rearrange("p g s e -> p (g s e)").bitcast(F32)[:, 0:NSEG * P].rearrange(
            "p (s e) -> p s e", s=NSEG)
        restart()
        hid = carve(NF, SEG)
        sg = carve(2, SEG)
        wx = carve(2 * 3, FF).rearrange("p (s k) f -> p s k f", s=2)
        xg = carve(2 * NB, ROW).rearrange("p (s b) c -> p s b c", s=2)
        xinT = carve(2, SEG)
        y = sb("y", [P, 2, NB, P])
        selscore = sb("selscore", [P, SEG])
        score = sb("score", [P, SEG])[:, :]
        tmp = sb("tmp", [P, 4, SEG])
        gt, eq, eqc, junk = (tmp[:, i, :] for i in range(4))
        sel, posc = eqc, junk
        ones1 = sb("ones1", [P, 1])
        ones_row = ones1[:, 0:1].to_broadcast([P, SEG])
        slot_i = tmp[:, 1:4, :].bitcast(I32)
        slot_f = gt.bitcast(F16)

        pG = [ps(f"pG{i}", [P, SEG]) for i in range(2)]
        pU = [ps(f"pU{i}", [P, SEG]) for i in range(2)]
        pY = ps("pY", [P, SEG])
        pO = ps("pO", [P, SEG])
        pR = [ps(f"pR{i}", [P, SEG]) for i in range(2)]

        const_loads = [
            (ident[:, :], d["ident"]), (vec[:, :], d["vec"]), (gate[:, :], d["gate"]),
            (w_rkvg[:, :, :], d["w_rkvg"]), (w_a[:, :], d["w_a"]), (w_b[:, :], d["w_b"]),
            (headones[:, :], d["headones"]), (segones[:, :], d["segones"]), (bits[:, :], d["bits"]),
            (center[:, :], d["center"]), (selc[:, :, :], d["selc"]), (sh_gu[:, :, :], d["sh_gu"]),
            (sh_dn[:, :, :], d["sh_dn"]), (headmean[:, :], d["headmean"]), (w_o[:, :], d["w_o"]),
            (w_f1[:, :], d["w_f1"]), (w_f2[:, :, :], d["w_f2"]), (seglow[:, :], d["seglow"]),
            (tokval[:, :], d["tokval"]), (iota[:, :], d["iota"]), (own4[:, :], d["own4"]), (ex_bias[:, :, :], d["ex_bias"]),
        ]
        NFIRST = 3
        x_loaded = [sem(f"x_loaded{i}") for i in range(4)]
        first_loaded = sem("first_loaded")
        consts_loaded = sem("consts_loaded")
        bias_loaded = sem("bias_loaded")
        bias_zeroed = sem("bias_zeroed")
        edges_ready = sem("edges_ready")
        stats_ready = sem("stats_ready")
        var_ready = sem("var_ready")
        pow_ready = sem("pow_ready")
        xn_ready = sem("xn_ready")
        hrow_ready = sem("hrow_ready")
        xnT_made = sem("xnT_made")
        hT_made = sem("hT_made")
        xnT_ready = sem("xnT_ready")
        hT_ready = sem("hT_ready")
        gate_ready = sem("gate_ready")
        logits_ready = sem("logits_ready")
        exp_ready = sem("exp_ready")

        def after(engine, sem, n):
            if not (isinstance(n, int) and n <= 0):
                engine.wait_ge(sem, n)
                if engine is nc.sync and not isinstance(n, int):
                    engine.nop(nofuse=True)

        def cols(ap, i):
            return ap[:, bass.ds(i, 1), :].rearrange("p o m -> p (o m)")

        QT = NT // 4
        POWERS = ((0, 0), (1, 0), (0, 1), (2, 0), (1, 1), (3, 0), (2, 1), (3, 1))

        def power(q, half):
            return POWERS.index((q, half)) + 1

        names = ("R", "K", "V", "A", "B", "C", "G", "O", "VAR", "WO", "H2", "F", "FO")
        made = {n: sem(f"{n}_made") for n in names}
        taken = {n: sem(f"{n}_taken") for n in names}
        BANK = {"VAR": 1, "R": 0, "K": 1, "V": 0, "A": 1, "B": 0, "WO": 1, "C": 0, "G": 1, "H2": 0, "FO": 1}
        F_BANK = (1, 0, 1, 0)
        xx = sb("xx", [P, SEG])[:, :]
        xx_ready = sem("xx_ready")
        mix_ready = sem("mix_ready")
        v_stored = sem("v_stored")
        v_spread = sem("v_spread")
        carried = sem("carried")
        kv_ready = sem("kv_ready")
        dec_made = sem("dec_made")
        dec_ready = sem("dec_ready")
        rcur_ready = sem("rcur_ready")
        gcur_ready = sem("gcur_ready")
        ruk_ready = sem("ruk_ready")
        scan_done = sem("scan_done")
        rs_ready = sem("rs_ready")
        rs_used = sem("rs_used")
        sq_ready = sem("sq_ready")
        rstd_ready = sem("rstd_ready")
        gn_ready = sem("gn_ready")
        og_ready = sem("og_ready")
        ms_ready = sem("ms_ready")
        mse_ready = sem("mse_ready")
        mpow_ready = sem("mpow_ready")
        h2_ready = sem("h2_ready")
        searched = sem("searched")
        count_ready = sem("count_ready")
        total_ready = sem("total_ready")
        linked = sem("linked")
        slot_ready = sem("slot_ready")
        slotT_ready = sem("slotT_ready")
        slotT_used = sem("slotT_used")
        onehot_ready = sem("onehot_ready")
        onehot_used = sem("onehot_used")
        list_ready = sem("list_ready")
        list_used = sem("list_used")
        idx_made = sem("idx_made")
        idx_ready = sem("idx_ready")
        selscore_ready = sem("selscore_ready")
        sum_set = [sem(f"sum_set{i}") for i in range(2)]
        sh_made = sem("sh_made")
        shs_ready = sem("shs_ready")
        shu_ready = sem("shu_ready")
        shared_hid_ready = sem("shared_hid_ready")
        pY_made = sem("pY_made")
        pY_taken = sem("pY_taken")
        w_loaded = [sem(f"w_loaded{i}") for i in range(2)]
        gathered = [sem(f"gathered{i}") for i in range(2)]
        idx_taken = sem("idx_taken")
        dram_written = sem("dram_written")
        gu_made = sem("gu_made")
        sg_ready = sem("sg_ready")
        hid_ready = sem("hid_ready")
        xT_made = sem("xT_made")
        xT_ready = sem("xT_ready")
        y_made = sem("y_made")
        y_ready = sem("y_ready")
        x_again = sem("x_again")

        LIST_PASS, LAST = SPB - 1, NSEG - 1
        PER = NBITS // 3
        SEARCH = ((0,), (1, 2), (3,), (4,), (5,), (6,), (7,), (8, 9))
        assert sum(len(t) for t in SEARCH) == PER
        EP = 4
        F0_, FO0, HID0, Y0, YM0 = 1, 1, 2, 2, 1
        TABLE = 16 * NSEG

        with nc.Block() as block:
            @block.sync
            def _(sp):
                def load_expert(e, buf):
                    sp.dma_start(wx[:, buf, 0:2, :], d["ex_gu"][bass.ds(e, 1)]
                                 .rearrange("o p a f -> (o p) a f")).then_inc(w_loaded[buf], 16)
                    sp.dma_start(wx[:, buf, 2, :], d["ex_dn"][bass.ds(e, 1)]
                                 .rearrange("o p f -> (o p) f")).then_inc(w_loaded[buf], 16)

                def spread_v(c):
                    after(sp, taken["V"], c + 1)
                    sp.dma_start(v_dram[:, :], v_sb).then_inc(v_stored, 16)
                    after(sp, v_stored, 16 * c + 16)
                    after(sp, kv_ready, DK * c)
                    sp.dma_start(vb.rearrange("p v t -> p (v t)"),
                                 v_dram[:, :].rearrange("(h v) t -> h (v t)", h=H).unsqueeze(1)
                                 .to_broadcast([H, DK, DK * SEG])).then_inc(v_spread, 16)

                def reload_x(p):
                    c = p * 2 - 8
                    for k in range(2):
                        if isinstance(p, int) and p == LAST and k == 1:
                            after(sp, taken["WO"], NSEG)
                        sp.dma_start(xa[:, bass.ds(c * NB + k * NB, NB), 0:D],
                                     d["x"][bass.ds(c * SEG + k * SEG, SEG), :]
                                     .rearrange("(b p) c -> p b c", p=P)).then_inc(x_again, 16)

                def experts(p, last):
                    for s in range(EP):
                        e = p * EP - 4 * EP + s
                        if not (last and s >= 2):
                            after(sp, y_made, e + 1 + YM0)
                            load_expert(e + 2, s % 2)

                xv = d["x"].rearrange("(q i p) c -> q p i c", p=P, q=4)
                for q in range(4):
                    sp.dma_start(x_in[:, QT * q:QT * q + QT, :], xv[q]).then_inc(x_loaded[q], 16)
                for i, (dst, src) in enumerate(const_loads):
                    sp.dma_start(dst, src).then_inc(first_loaded if i < NFIRST else consts_loaded, 16)
                sp.wait_ge(bias_zeroed, 1)
                for s in range(NSEG):
                    sp.dma_start(down_b[s * E:(s + 1) * E, s, :], d["down_b"]).then_inc(bias_loaded, 16)
                sp.wait_ge(xn_ready, NT)
                spread_v(0)
                spread_v(1)
                with sp.Fori(1, 3) as p:
                    spread_v(p + 1)
                spread_v(4)
                for c in range(NSEG):
                    sp.wait_ge(pY_taken, 8 + c)
                    sp.dma_start(moe_sum[c * SEG:(c + 1) * SEG, :].rearrange("(b p) c -> p b c", p=P),
                                 y[:, c % 2, :, :]).then_inc(sum_set[c % 2], 16)
                sp.wait_ge(list_ready, 1)
                load_expert(0, 0)
                load_expert(1, 1)
                sp.wait_ge(dram_written, TABLE)
                with sp.Fori(4, 6) as p:
                    spread_v(p + 1)
                    experts(p, False)
                    reload_x(p)
                spread_v(7)
                experts(6, False)
                reload_x(6)
                experts(7, True)
                reload_x(7)
                sp.wait_ge(x_again, 16 * NSEG)

            @block.gpsimd
            def _(pool):
                G = nc.gpsimd

                def diff(c):
                    after(pool, mix_ready, 5 * c)
                    G.tensor_tensor(xx, cols(hT[:, :, 0:SEG], c), cols(hT[:, :, 1:SEG + 1], c),
                                    ALU.subtract).then_inc(xx_ready, 1)

                def kv(c, i, carry):
                    if carry is not None:
                        after(pool, rs_ready, DK * (c - 1) + i + 1)
                    if carry == "copy":
                        pool.nop(nofuse=True)
                        G.tensor_copy(kvS[:, i, 0:1], kvS[:, i, SEG:SEG + 1]).then_inc(carried, 1)
                    else:
                        G.memset(kvS[:, i, 0:1], 0.0).then_inc(carried, 1)
                    after(pool, carried, DK * c + i + 1)
                    if i == 0:
                        after(pool, v_spread, 16 * c + 16)
                        after(pool, taken["K"], c + 1)
                    G.tensor_tensor(kvS[:, i, 1:SEG + 1], vb[:, i, :], k_sb, ALU.mult).then_inc(kv_ready, 1)

                def gate_out(c):
                    after(pool, gn_ready, c + 1)
                    after(pool, gcur_ready, c + 1)
                    G.tensor_tensor(og, og, g_cur, ALU.mult).then_inc(og_ready, 1)

                def rms_pow(c):
                    after(pool, mse_ready, c + 1)
                    G.tensor_tensor(ms[:, 2, :], ms[:, 1, :], minus_half[:, 0:NB], ALU.pow).then_inc(mpow_ready, 1)

                def gather(e, s):
                    G.tensor_copy(idx_e[:, s, :], idx[:, bass.ds(e * NB, NB)]).then_inc(idx_taken, 1)
                    pool.wait_ge(idx_taken, e + 1)
                    pool.nop(nofuse=True)
                    for q in range(NB):
                        G.indirect_dma_start(xg[:, s % 2, q, :], None, rows[:, :],
                                             bass.IndirectOffsetOnAxis(ap=idx_e[:, s, q:q + 1], axis=0)
                                             ).then_inc(gathered[s % 2], 16)

                def scatter(e, s):
                    after(pool, dram_written, e * 16 * NB + TABLE)
                    pool.nop(nofuse=True)
                    for q in range(NB):
                        G.indirect_dma_start(moe_sum[:, :],
                                             bass.IndirectOffsetOnAxis(ap=idx_e[:, s, q:q + 1], axis=0),
                                             y[:, s % 2, q, :], None, compute_op=ALU.add).then_inc(dram_written, 16)

                def store_table():
                    pool.wait_ge(slotT_used, 2)
                    rv = rows[:, :].rearrange("(q i p) c -> q p i c", p=P, q=NSEG)
                    for q in range(NSEG):
                        G.dma_start(rv[q], xa[:, NB * q:NB * q + NB, :]).then_inc(dram_written, 16)

                def first_row(p):
                    first = isinstance(p, int) and p == 0
                    diff(p + 2)
                    if not first:
                        gate_out(p - 1)
                    shared_step(p, 0, 0)
                    carry = "zero" if isinstance(p, int) and p == LIST_PASS else "copy"
                    shared_step(p, 0, 1)
                    if carry == "zero":
                        rms_pow(p - 1)
                        store_table()
                    for i in range(DK):
                        kv(p + 1, i, carry)
                        if i == 2 and not first and carry == "copy":
                            rms_pow(p - 1)
                        if i == 4 and carry == "zero":
                            pool.wait_ge(idx_ready, 1)
                            pool.wait_ge(dram_written, TABLE)
                            gather(0, 0)
                        if i in (4, 5):
                            shared_step(p, 1, i - 4)
                        if i == 7 and carry == "zero":
                            gather(1, 1)

                def shared_step(p, half, f):
                    n = p * 4 + 2 * half + f
                    after(pool, shs_ready, n + 1)
                    after(pool, shu_ready, n + 1)
                    G.tensor_tensor(shs[:, f, :], shs[:, f, :], shu[:, f, :], ALU.mult).then_inc(shared_hid_ready, 1)

                def turn_over(p, s):
                    e = p * EP - 4 * EP + s
                    after(pool, y_ready, e + 1 + Y0)
                    if not (isinstance(p, int) and p == LAST and s >= 2):
                        gather(e + 2, (s + 2) % 4)
                    scatter(e, s)

                def second_row(p, mixes):
                    if mixes:
                        diff(p + 2)
                    gate_out(p - 1)
                    turn_over(p, 0)
                    for i in range(DK):
                        kv(p + 1, i, "copy")
                        if i == 2:
                            rms_pow(p - 1)
                            turn_over(p, 1)
                        if i == 5:
                            turn_over(p, 2)
                    turn_over(p, 3)

                def last_row(p):
                    gate_out(p - 1)
                    rms_pow(p - 1)
                    turn_over(p, 0)
                    turn_over(p, 1)
                    gate_out(p)
                    turn_over(p, 2)
                    rms_pow(p)
                    turn_over(p, 3)

                nc.gpsimd.memset(down_b, 0.0).then_inc(bias_zeroed, 1)
                for k, (q, half) in enumerate(POWERS):
                    pool.wait_ge(var_ready, k + 1)
                    G.tensor_tensor(small[:, 2 * half + 1, QT * q:QT * q + QT],
                                    small[:, 2 * half, QT * q:QT * q + QT],
                                    minus_half[:, 0:QT], ALU.pow).then_inc(pow_ready, 1)
                    if (q, half) == (2, 0):
                        pool.wait_ge(hT_ready, 1)
                        diff(0)
                pool.wait_ge(hT_made, NSEG)
                pool.wait_ge(edges_ready, 1)
                diff(1)
                for i in range(DK):
                    kv(0, i, None)
                first_row(0)
                with pool.Fori(1, 3) as p:
                    first_row(p)
                first_row(LIST_PASS)
                for t in sum_set:
                    pool.wait_ge(t, 16 * NSEG // 2)
                with pool.Fori(4, 6) as p:
                    second_row(p, True)
                second_row(6, False)
                last_row(LAST)
                pool.wait_ge(dram_written, 16 * NB * E + TABLE)

            @block.vector
            def _(v):
                V = nc.vector

                def mixes(c, which):
                    for m in which:
                        after(v, xx_ready, c + 1)
                        after(v, made[("R", "K", "V", "G", "A")[m]], c)
                        V.scalar_tensor_tensor(mix[:, m, :], xx, vec[:, MUS[m]:MUS[m] + 1],
                                               cols(hT[:, :, 1:SEG + 1], c), ALU.mult, ALU.add).then_inc(mix_ready, 1)

                def scan(c, i):
                    after(v, kv_ready, DK * c + i + 1)
                    if i == 0:
                        after(v, dec_ready, c + 1)
                    V.tensor_tensor_scan(kvS[:, i, 1:SEG + 1], dec, kvS[:, i, 1:SEG + 1], kvS[:, i, 0:1],
                                         ALU.mult, ALU.add).then_inc(scan_done, 1)

                def r_state(c, i):
                    after(v, scan_done, DK * c + i + 1)
                    if i == 0:
                        after(v, rcur_ready, c + 1)
                    if i == 1:
                        after(v, made["O"], c)
                    else:
                        after(v, rs_used, c * (DK - 1) + max(i - 1, 0))
                    V.tensor_tensor(rs[:, i % 2, :], r_cur, kvS[:, i, 0:SEG], ALU.mult).then_inc(rs_ready, 1)

                def weigh_own(c):
                    after(v, taken["R"], c + 1)
                    after(v, taken["K"], c + 1)
                    after(v, made["C"], c)
                    V.scalar_tensor_tensor(ruk, r_next, vec[:, U:U + 1], k_sb, ALU.mult, ALU.mult).then_inc(ruk_ready, 1)

                def own(c):
                    after(v, made["C"], c + 1)
                    V.tensor_tensor(cv, pR[BANK["C"]][:, :], v_sb, ALU.mult).then_inc(taken["C"], 1)

                def normalise(c):
                    after(v, rstd_ready, c + 1)
                    V.tensor_tensor(og, pO[:, :], og, ALU.mult).then_inc(taken["O"], 1)

                def residual(c):
                    after(v, made["WO"], c + 1)
                    V.tensor_tensor(x2[:, :, :], pR[BANK["WO"]][:, :].rearrange("p (b c) -> p b c", b=NB),
                                    xa[:, bass.ds(c * NB, NB), 0:D], ALU.add).then_inc(taken["WO"], 1)
                    after(v, taken["WO"], c + 1)
                    for b in range(NB):
                        V.tensor_tensor_reduce(h2[:, b, :], x2[:, b, :], x2[:, b, :], 1.0, 0.0, ALU.mult, ALU.add,
                                               ms[:, 0, b:b + 1]).then_inc(ms_ready, 1)
                    after(v, ms_ready, c * NB + NB)
                    V.tensor_scalar(ms[:, 1, :], ms[:, 0, :], 1.0 / D, EPS_RMS, ALU.mult, ALU.add).then_inc(mse_ready, 1)

                def rms(c):
                    after(v, mpow_ready, c + 1)
                    V.tensor_tensor(h2[:, :, :], x2[:, :, :], ms[:, 2, :].unsqueeze(2).to_broadcast([P, NB, P]),
                                    ALU.mult).then_inc(h2_ready, 1)

                def block_out(c):
                    after(v, made["FO"], c + 1)
                    V.tensor_tensor(cols(hT[:, :, 0:SEG], c).rearrange("p (b c) -> p b c", b=NB),
                                    pR[BANK["FO"]][:, :].rearrange("p (b c) -> p b c", b=NB), x2[:, :, :],
                                    ALU.add).then_inc(taken["FO"], 1)

                def update(j):
                    after(v, total_ready, j)
                    V.scalar_tensor_tensor(kept[:, :], pU[1][:, 0:1], CAP - 0.5, cand[:, :],
                                           ALU.is_ge, ALU.mult).then_inc(searched, 1)
                    after(v, searched, j * 3 - 1)
                    V.tensor_tensor(cur[:, :], cur[:, :], kept[:, :], ALU.max).then_inc(searched, 1)
                    after(v, searched, j * 3)

                def search_step(j):
                    if not (isinstance(j, int) and j == 0):
                        update(j)
                    V.tensor_tensor(cand[:, :].bitcast(I32), cur[:, :].bitcast(I32), bits[:, bass.ds(j, 1)],
                                    ALU.bitwise_or).then_inc(searched, 1)
                    after(v, searched, j * 3 + 1)
                    V.tensor_scalar(gt, score, cand[:, :], None, ALU.is_ge, ALU.add,
                                    accum_out=cnt[:, 0:1]).then_inc(count_ready, 1)

                link = Count(linked, v)

                def choose():
                    update(NBITS)
                    link.sig(V.tensor_scalar(gt, score, cur[:, :], None, ALU.is_gt, ALU.add, accum_out=cnt[:, 0:1]))
                    link.step(V.tensor_scalar(eq, score, cur[:, :], None, ALU.is_equal, ALU.add,
                                              accum_out=cnt[:, 1:2]))
                    V.tensor_tensor_scan(eqc, ones_row, eq, 0.0, ALU.mult, ALU.add).then_inc(count_ready, 1)

                def number():
                    v.wait_ge(total_ready, NBITS + 1)
                    link.step(V.tensor_scalar(lim[:, 0:1], pU[1][:, 0:1], -1.0, float(CAP), ALU.mult, ALU.add))
                    link.step(V.tensor_tensor(lim[:, 1:2], lim[:, 0:1], pU[1][:, 3:4], ALU.subtract))
                    link.step(V.scalar_tensor_tensor(eqc, eqc, lim[:, 1:2], eq, ALU.is_le, ALU.mult))
                    link.step(V.tensor_tensor(sel, eqc, gt, ALU.add))
                    link.step(V.tensor_tensor_scan(posc, ones_row, sel, 0.0, ALU.mult, ALU.add))
                    V.tensor_copy(cnt[:, 2:3], posc[:, SEG - 1:SEG]).then_inc(count_ready, 1)
                    V.tensor_tensor(selscore[:, :], sel, score, ALU.mult).then_inc(selscore_ready, 1)
                    link.step(V.scalar_tensor_tensor(eq, sel, -float(TOK), posc, ALU.mult, ALU.add))

                def place():
                    v.wait_ge(total_ready, NBITS + 2)
                    link.step(V.tensor_scalar(lim[:, 0:1], pU[1][:, 4:5], TOK - 1.0, None, ALU.add))
                    V.tensor_scalar(gt, eq, lim[:, 0:1], None, ALU.add).then_inc(slot_ready, 1)

                def turn():
                    v.wait_ge(slotT_ready, 1)
                    V.tensor_copy(slot_i[:, 0, :], pG[0][:, :]).then_inc(slotT_used, 1)
                    for b in range(NB):
                        ins = V.tensor_copy(xa[:, :, D:ROW].rearrange("p (s b) e -> p b s e", b=NB)[:, b],
                                            pG[1][:, b * P:(b + 1) * P].rearrange("p (s e) -> p s e", e=E))
                    ins.then_inc(slotT_used, 1)
                    v.wait_ge(slotT_used, 1)
                    link.sig(V.tensor_scalar(slot_i[:, 1, :], slot_i[:, 0, :], 4, None, ALU.logical_shift_right))
                    link.step(V.tensor_scalar(slot_i[:, 2, :], slot_i[:, 0, :], SLOW - 1, None, ALU.bitwise_and))
                    link.sig(V.tensor_copy(slot_f[:, 0:NB * P], slot_i[:, 1, :]))
                    link.step(V.tensor_copy(slot_f[:, NB * P:2 * NB * P], slot_i[:, 2, :]))

                def onehots(half):
                    if half:
                        v.wait_ge(onehot_used, 1)
                    t = slice(half * HT, (half + 1) * HT)

                    def spread(row, values):
                        return row.rearrange("p (g e) -> p g e", e=4).unsqueeze(2).to_broadcast(
                            [P, HT // 4, values, 4])

                    def ramp(values):
                        return iota[:, 0:4 * values].rearrange("p (s e) -> p s e", e=4).unsqueeze(1).to_broadcast(
                            [P, HT // 4, values, 4])

                    link.step(V.tensor_tensor(one_b, spread(slot_f[:, NB * P:2 * NB * P][:, t], SLOW), ramp(SLOW),
                                              ALU.is_equal))
                    V.tensor_tensor(one_a, spread(slot_f[:, t], SHIGH), ramp(SHIGH), ALU.is_equal)
                    V.tensor_tensor(one_b, one_b, spread(tokval[:, t], SLOW), ALU.mult).then_inc(onehot_ready, 1)

                def list_out():
                    v.wait_ge(list_ready, 1)
                    both = pU[1][:, 0:256].rearrange("p (g b f) -> p g f b", g=4, f=4)
                    link.step(V.tensor_scalar(list_ab, both[:, :, 0, :], own4[:, 0:1], None, ALU.mult))
                    for e4 in (1, 2):
                        link.step(V.scalar_tensor_tensor(list_ab, both[:, :, e4, :], own4[:, e4:e4 + 1], list_ab,
                                                         ALU.mult, ALU.add))
                    V.scalar_tensor_tensor(list_ab, both[:, :, 3, :], own4[:, 3:4], list_ab,
                                           ALU.mult, ALU.add).then_inc(list_used, 1)

                def idx_out():
                    v.wait_ge(idx_made, 1)
                    for e4 in range(4):
                        ins = V.tensor_scalar(
                            idx[:, :].rearrange("p (g f q) -> p g f q", g=4, f=4)[:, :, e4, :],
                            (pG + pU)[e4][:, 0:16].rearrange("p (g q) -> p g q", g=4), TOK / 2.0, None, ALU.add)
                    ins.then_inc(idx_ready, 1)

                def hid_step(e, f):
                    after(v, sg_ready, e * NF + f + 1)
                    after(v, y_made, e + YM0)
                    V.scalar_tensor_tensor(hid[:, f, :], pU[f % 2][:, :], ex_bias[:, 1, bass.ds(e * NF + f, 1)],
                                           sg[:, f % 2, :], ALU.add, ALU.mult).then_inc(hid_ready, 1)

                def scale_y(e, s):
                    after(v, y_made, e + 1 + YM0)
                    after(v, dram_written, e * 16 * NB - 16 * NB + TABLE)
                    V.tensor_tensor(y[:, s % 2, :, :], pY[:, :].rearrange("p (b c) -> p b c", b=NB),
                                    xg[:, s % 2, :, bass.ds(e + D, 1)].to_broadcast([P, NB, P]),
                                    ALU.mult).then_inc(y_ready, 1)

                def scores():
                    v.wait_ge(exp_ready, 1)
                    link.step(V.tensor_scalar(junk, gt, 1.0, None, ALU.add))
                    link.step(V.reciprocal(score, junk))

                def column(p, i):
                    scan(p, i)
                    r_state(p, i)

                def pass_(p, searching=False, listing=False, experts=False, finish=True, mixing=True):
                    for i in range(DK):
                        e = p * EP - 4 * EP + i // 2
                        f = 2 * (i % 2)
                        if listing and i == 2:
                            turn()
                        for k in ((0,), (), (2, 3), (4,), (5,), (6,), (7,), ())[i] if listing else (i,):
                            scan(p, k)
                            if searching and i:
                                search_step(p * PER + SEARCH[i][0])
                            r_state(p, k)
                        if searching and i == 0:
                            if isinstance(p, int) and p == 0:
                                own(0)
                                scores()
                            search_step(p * PER)
                        if experts:
                            hid_step(e, f)
                            hid_step(e, f + 1)
                        if i == (0 if experts else 1) and finish and not listing:
                            normalise(p - 1)
                        if i == 2:
                            weigh_own(p + 1)
                        if i == (2 if listing else 3) and finish:
                            residual(p - 1)
                        if i == (3 if listing else 4):
                            own(p + 1)
                            if finish:
                                rms(p - 1)
                        if mixing and i >= 4:
                            mixes(p + 2, ((MIX_R,), (MIX_K,), (MIX_V, MIX_G), (MIX_W,))[i - 4])
                        if searching and len(SEARCH[i]) == 2:
                            search_step(p * PER + SEARCH[i][1])
                        if listing and i == 0:
                            choose()
                            normalise(p - 1)
                            column(p, 1)
                            number()
                        if listing and i == 1:
                            place()
                        if listing and i == 2:
                            onehots(0)
                        if listing and i == 3:
                            onehots(1)
                        if listing and i == 4:
                            list_out()
                            idx_out()
                        if experts and i % 2 == 1:
                            scale_y(e, i // 2)
                    if finish:
                        block_out(p - 1)

                def last_pass(p):
                    for i in range(DK):
                        e = p * EP - 4 * EP + i // 2
                        f = 2 * (i % 2)
                        c = p - 1 + i // 4
                        if i < 4:
                            column(p, 2 * i)
                        hid_step(e, f)
                        if i < 4:
                            column(p, 2 * i + 1)
                        hid_step(e, f + 1)
                        if i in (0, 5):
                            normalise(c)
                        if i in (1, 6):
                            residual(c)
                        if i in (2, 6):
                            rms(c)
                        if i % 2 == 1:
                            scale_y(e, i // 2)
                        if i % 4 == 3:
                            block_out(c)

                for k, (s, n) in enumerate(((taken["FO"], FO0), (hid_ready, HID0), (y_ready, Y0))):
                    V.memset(cnt[:, k:k + 1], 0.0).then_inc(s, n)
                V.memset(ones1[:, :], 1.0)
                link.sig(V.memset(minus_half[:, :], -0.5))
                link.sig(V.memset(hT[:, :, 0:1], 0.0))
                link.sig(V.memset(cur[:, :], 0.0))
                link.step(V.memset(gate_pad, 0.0))
                v.wait_ge(y_ready, Y0)

                def moments(q):
                    v.wait_ge(x_loaded[q], 16)
                    for i in range(QT * q, QT * q + QT):
                        V.bn_stats(stats[:, i, :], x_in[:, i, :]).then_inc(stats_ready, 1)
                    v.wait_ge(stats_ready, QT * (q + 1))
                    for i in range(QT * q, QT * q + QT):
                        link.sig(V.bn_aggr(mv[:, i, :], stats[:, i, :]))
                    v.wait_ge(linked, link.n)
                    V.tensor_scalar(small[:, 0, QT * q:QT * q + QT], mv[:, QT * q:QT * q + QT, 1], EPS_LN, None,
                                    ALU.add).then_inc(var_ready, 1)

                def norm(q):
                    v.wait_ge(pow_ready, power(q, 0))
                    t = slice(QT * q, QT * q + QT)
                    link.step(V.tensor_tensor(small[:, 4, t], mv[:, t, 1], small[:, 1, t], ALU.mult))
                    link.step(V.tensor_tensor(small[:, 5, t], small[:, 4, t], small[:, 1, t], ALU.mult))
                    V.tensor_scalar(small[:, 2, t], small[:, 5, t], EPS_RMS, None, ALU.add).then_inc(var_ready, 1)
                    for i in range(QT * q, QT * q + QT):
                        V.tensor_scalar(xa[:, i, 0:D], x_in[:, i, :], mv[:, i, 0:1], small[:, 1, i:i + 1],
                                        ALU.subtract, ALU.mult).then_inc(xn_ready, 1)

                def copy_xnT(s):
                    v.wait_ge(xnT_made, s + 1)
                    V.tensor_copy(xnT[:, s, :], pG[s % 2][:, :]).then_inc(xnT_ready, 1)

                moments(0)
                moments(1)
                norm(0)
                moments(2)
                norm(1)
                copy_xnT(0)
                copy_xnT(1)
                mixes(0, (MIX_V,))
                v.wait_ge(first_loaded, 16 * NFIRST)
                for s in range(NSEG):
                    ins = V.tensor_copy(gate_pad[:, s, s * E:(s + 1) * E], gate[:, :])
                ins.then_inc(gate_ready, 1)
                moments(3)
                norm(2)
                norm(3)
                copy_xnT(2)
                copy_xnT(3)
                mixes(0, (MIX_R, MIX_K, MIX_G, MIX_W))
                copy_xnT(4)
                copy_xnT(5)
                weigh_own(0)
                copy_xnT(6)
                copy_xnT(7)
                v.wait_ge(hT_ready, NSEG)
                hb = hT[:, :, :].rearrange("p (b c) t -> p b c t", b=B)
                for b in range(B):
                    ins = V.tensor_copy(hb[:, b, 1:SPB, 0], hb[:, b, 0:SPB - 1, SEG])
                ins.then_inc(edges_ready, 1)
                mixes(1, (MIX_R, MIX_K, MIX_V, MIX_G, MIX_W))
                v.wait_ge(consts_loaded, 16 * (len(const_loads) - NFIRST))
                pass_(0, searching=True, finish=False)
                with v.Fori(1, 3) as p:
                    pass_(p, searching=True)
                pass_(LIST_PASS, listing=True)
                for t in sum_set:
                    v.wait_ge(t, 16 * NSEG // 2)
                with v.Fori(4, 6) as p:
                    pass_(p, experts=True)
                pass_(6, experts=True, mixing=False)
                last_pass(LAST)

            @block.scalar
            def _(act):
                A = nc.scalar

                def take(name, c, out, func, **kw):
                    after(act, made[name], c + 1)
                    return A.activation(out, pR[BANK[name]][0:out.shape[0], :], func, **kw).then_inc(taken[name], 1)

                def step_up(c):
                    after(act, rs_ready, DK * c)
                    after(act, taken["R"], c + 1)
                    A.activation(r_cur, r_next, ACT.Copy).then_inc(rcur_ready, 1)
                    after(act, dec_made, c * 2 + 2)
                    A.activation(dec, ew, ACT.Copy).then_inc(dec_ready, 1)

                def squares(c):
                    after(act, made["O"], c + 1)
                    A.activation(og, pO[:, :], ACT.Square).then_inc(sq_ready, 1)

                def log_var(c):
                    take("VAR", c, og, ACT.Ln, bias=vec[:, EPSG:EPSG + 1])

                def rstd(c):
                    after(act, taken["VAR"], c + 1)
                    A.activation(og, og, ACT.Exp, scale=-0.5).then_inc(rstd_ready, 1)

                def take_r(c):
                    after(act, ruk_ready, c)
                    after(act, rcur_ready, c)
                    take("R", c, r_next, ACT.Copy)

                def take_k(c):
                    after(act, kv_ready, DK * c)
                    take("K", c, k_sb, ACT.Copy)

                def take_v(c):
                    after(act, taken["C"], c)
                    after(act, v_stored, 16 * c)
                    take("V", c, v_sb, ACT.Copy)

                def scale_norm(c):
                    after(act, taken["O"], c + 1)
                    A.activation(og, og, ACT.Identity, scale=vec[:, GNW:GNW + 1],
                                 bias=vec[:, GNB:GNB + 1]).then_inc(gn_ready, 1)

                def tanh(c):
                    after(act, dec_ready, c)
                    take("A", c, ew[0:LORA, :], ACT.Tanh)

                def decay(c):
                    after(act, made["B"], c + 1)
                    A.activation(ew, pR[BANK["B"]][:, :], ACT.Exp, bias=vec[:, W0:W0 + 1]).then_inc(dec_made, 1)
                    after(act, dec_made, c * 2 + 1)
                    A.activation(ew, ew, ACT.Exp, scale=-1.0).then_inc(dec_made, 1)

                def gate_next(c):
                    if not (isinstance(c, int) and c == 0):
                        after(act, og_ready, c - 1)
                        after(act, taken["G"], c)
                        A.activation(g_cur, g_next, ACT.Copy).then_inc(gcur_ready, 1)
                        after(act, gcur_ready, c)
                    take("G", c, g_next, ACT.Silu)

                def h2_out(c):
                    take("H2", c, h2T[:, :], ACT.Copy, scale=vec[:, LN2:LN2 + 1])

                def gelu(c, f):
                    after(act, made["F"], c * NF + f + 1)
                    A.activation(gl[:, f, :], pR[F_BANK[f]][:, :], ACT.Gelu).then_inc(taken["F"], 1)

                def shared_step(p, half, f):
                    n = p * 4 + half * 2 + f
                    after(act, pY_made, p * 2 + half)
                    after(act, sh_made, n + 1)
                    A.activation(shs[:, f, :], pG[f][:, :], ACT.Silu).then_inc(shs_ready, 1)
                    A.activation(shu[:, f, :], pU[0][:, :], ACT.Copy).then_inc(shu_ready, 1)

                def shared_out(c, n):
                    after(act, pY_made, n)
                    A.activation(cols(xnT[:, :, :], c), pY[:, :], ACT.Copy).then_inc(pY_taken, 1)

                def bias_out(c):
                    after(act, pY_made, 8 + c)
                    if c >= 2:
                        after(act, sum_set[c % 2], 16 * (c // 2))
                    A.activation(y[:, c % 2, :, :], pY[:, :].rearrange("p (b c) -> p b c", b=NB),
                                 ACT.Copy).then_inc(pY_taken, 1)

                def silu_step(e, f):
                    after(act, gu_made, e * NF + f + 1)
                    A.activation(sg[:, f % 2, :], pG[f % 2][:, :], ACT.Silu,
                                 bias=ex_bias[:, 0, bass.ds(e * NF + f, 1)]).then_inc(sg_ready, 1)

                def x_out(e, s):
                    after(act, xT_made, e + 1)
                    A.activation(xinT[:, s % 2, :], pY[:, :], ACT.Copy).then_inc(xT_ready, 1)

                def first_row(p, finish, listing=False):
                    take_r(p + 1)
                    if finish:
                        log_var(p - 1)
                    if finish:
                        rstd(p - 1)
                    take_v(p + 1)
                    take_k(p + 1)
                    if finish:
                        scale_norm(p - 1)
                    shared_step(p, 0, 0)
                    tanh(p + 1)
                    if not listing:
                        shared_step(p, 0, 1)
                    decay(p + 1)
                    if listing:
                        shared_step(p, 0, 1)
                        shared_out(p * 2, p * 2 + 1)
                        bias_out(0)
                        bias_out(1)
                    gate_next(p + 1)
                    if listing:
                        h2_out(p - 1)
                        for f in range(NF):
                            bias_out(2 + f)
                            gelu(p - 1, f)
                        bias_out(6)
                    else:
                        shared_out(p * 2, p * 2 + 1)
                    shared_step(p, 1, 0)
                    if finish and not listing:
                        h2_out(p - 1)
                    shared_step(p, 1, 1)
                    if listing:
                        bias_out(7)
                    if finish and not listing:
                        for f in range(NF):
                            gelu(p - 1, f)
                    step_up(p + 1)
                    squares(p)
                    shared_out(p * 2 + 1, 16 if listing else p * 2 + 2)

                def second_row(p):
                    for i in range(DK):
                        e = p * EP - 4 * EP + i // 2
                        f = 2 * (i % 2)
                        silu_step(e, f)
                        silu_step(e, f + 1)
                        if i % 2 == 1 and i > 1:
                            x_out(e + 1, i // 2 + 1)
                        if i == 0:
                            take_r(p + 1)
                            log_var(p - 1)
                            rstd(p - 1)
                            scale_norm(p - 1)
                        if i == 1:
                            take_v(p + 1)
                            take_k(p + 1)
                            x_out(e + 1, 1)
                        if i == 2:
                            tanh(p + 1)
                        if i == 3:
                            decay(p + 1)
                        if i == 4:
                            gate_next(p + 1)
                        if i == 5:
                            h2_out(p - 1)
                        if i == 7:
                            for k in range(NF):
                                gelu(p - 1, k)
                            step_up(p + 1)
                            squares(p)

                def last_row(p):
                    for i in range(DK):
                        e = p * EP - 4 * EP + i // 2
                        f = 2 * (i % 2)
                        c = p - 1 + i // 4
                        if i == 4:
                            squares(c)
                        silu_step(e, f)
                        silu_step(e, f + 1)
                        if i % 2 == 1 and i < 7:
                            x_out(e + 1, i // 2 + 1)
                        if i in (0, 5):
                            log_var(c)
                            rstd(c)
                            scale_norm(c)
                        if i == 2:
                            after(act, og_ready, c + 1)
                            after(act, taken["G"], NSEG)
                            A.activation(g_cur, g_next, ACT.Copy).then_inc(gcur_ready, 1)
                        if i % 4 == 3:
                            h2_out(c)
                            for k in range(NF):
                                gelu(c, k)

                act.wait_ge(first_loaded, 16 * NFIRST)
                for _ in range(F0_):
                    A.activation(g_cur[:, 0:1], vec[:, 0:1], ACT.Copy).then_inc(taken["F"], 1)
                def first_rows(q):
                    act.wait_ge(pow_ready, power(q, 1))
                    act.wait_ge(xn_ready, QT * (q + 1))
                    for i in range(QT * q, QT * q + QT):
                        A.activation(hrow[:, i, :], xa[:, i, 0:D], ACT.Copy,
                                     scale=small[:, 3, i:i + 1]).then_inc(hrow_ready, 1)

                def first_out(q):
                    for s in (2 * q, 2 * q + 1):
                        act.wait_ge(hT_made, s + 1)
                        A.activation(hT[:, s, 1:SEG + 1], pU[s % 2][:, :], ACT.Copy,
                                     scale=vec[:, LN1:LN1 + 1]).then_inc(hT_ready, 1)

                first_rows(0)
                first_out(0)
                first_rows(1)
                take_v(0)
                first_out(1)
                first_rows(2)
                first_rows(3)
                first_out(2)
                take_r(0)
                take_k(0)
                first_out(3)
                tanh(0)
                decay(0)
                step_up(0)
                act.wait_ge(logits_ready, 1)
                A.activation(gt, pY[:, :], ACT.Exp, scale=-1.0).then_inc(exp_ready, 1)
                gate_next(0)
                act.wait_ge(consts_loaded, 16 * (len(const_loads) - NFIRST))
                first_row(0, False)
                with act.Fori(1, 3) as p:
                    first_row(p, True)
                first_row(LIST_PASS, True, True)
                x_out(0, 0)
                with act.Fori(4, 7) as p:
                    second_row(p)
                last_row(LAST)

            @block.tensor
            def _(pe):
                X = nc.tensor

                def proj(name, m, c, *before, mixed=None):
                    for s, n in before:
                        after(pe, s, n)
                    after(pe, mix_ready, 5 * c + m + 1 if mixed is None else mixed)
                    w = w_a[:, :] if name == "A" else w_rkvg[:, m, :]
                    o = pR[BANK[name]]
                    X.matmul(o[0:LORA, :] if name == "A" else o[:, :], w, mix[:, m, :], start=True,
                             stop=True).then_inc(made[name], 1)

                def lora_out(c, *before):
                    for s, n in before:
                        after(pe, s, n)
                    after(pe, taken["V"], c + 1)
                    after(pe, taken["A"], c + 1)
                    X.matmul(pR[BANK["B"]][:, :], w_b[:, :], ew[0:LORA, :], start=True, stop=True
                             ).then_inc(made["B"], 1)

                def own(c):
                    after(pe, dec_made, c * 2 + 1)
                    after(pe, ruk_ready, c + 1)
                    X.matmul(pR[BANK["C"]][:, :], headones[:, :], ruk, start=True, stop=True).then_inc(made["C"], 1)

                def open_o(c):
                    after(pe, taken["O"], c)
                    after(pe, taken["C"], c + 1)
                    X.matmul(pO[:, :], center[:, :], cv, start=True, stop=False)

                def add_o(c, i):
                    after(pe, rs_ready, DK * c + i + 1)
                    ins = X.matmul(pO[:, :], selc[:, i, :], rs[:, i % 2, :], start=False, stop=(i == DK - 1))
                    ins.then_inc(made["O"] if i == DK - 1 else rs_used, 1)

                def var(c):
                    after(pe, taken["FO"], c + FO0)
                    if not (isinstance(c, int) and c == LAST):
                        after(pe, taken["G"], c + 2)
                    after(pe, sq_ready, c + 1)
                    X.matmul(pR[BANK["VAR"]][:, :], headmean[:, :], og, start=True, stop=True).then_inc(made["VAR"], 1)

                def w_out(c, *before):
                    for s, n in before:
                        after(pe, s, n)
                    after(pe, og_ready, c + 1)
                    for b in range(NB):
                        ins = X.matmul(pR[BANK["WO"]][:, b * P:(b + 1) * P], og[:, b * P:(b + 1) * P], w_o[:, :],
                                       start=True, stop=True)
                    ins.then_inc(made["WO"], 1)

                def turn_h2(c, *before):
                    for s, n in before:
                        after(pe, s, n)
                    after(pe, h2_ready, c + 1)
                    for b in range(NB):
                        ins = X.transpose(pR[BANK["H2"]][:, b * P:(b + 1) * P], h2[:, b, :], ident[:, :])
                    ins.then_inc(made["H2"], 1)

                def ff1(c, f, *before):
                    for s, n in before:
                        after(pe, s, n)
                    if f == 0:
                        after(pe, taken["H2"], c + 1)
                    if f >= 2:
                        after(pe, taken["F"], c * NF + f - 1 + F0_)
                    X.matmul(pR[F_BANK[f]][:, :], w_f1[:, f * P:(f + 1) * P], h2T[:, :], start=True, stop=True
                             ).then_inc(made["F"], 1)

                def ff2(c):
                    after(pe, taken["F"], c * NF + NF + F0_)
                    for b in range(NB):
                        for f in range(NF):
                            ins = X.matmul(pR[BANK["FO"]][:, b * P:(b + 1) * P], gl[:, f, b * P:(b + 1) * P],
                                           w_f2[:, f, :], start=(f == 0), stop=(f == NF - 1))
                    ins.then_inc(made["FO"], 1)

                def shared_up(p, half, f):
                    n = p * 4 + half * 2 + f
                    after(pe, shs_ready, n - 1)
                    after(pe, shu_ready, n)
                    if isinstance(p, int) and p == LIST_PASS:
                        if (half, f) == (0, 1):
                            pe.wait_ge(slotT_used, 2)
                        if (half, f) == (1, 0):
                            pe.wait_ge(idx_ready, 1)
                    rhs = cols(xnT[:, :, :], p * 2 + half)
                    X.matmul(pG[f][:, :], sh_gu[:, 0, f * P:(f + 1) * P], rhs, start=True, stop=True)
                    X.matmul(pU[0][:, :], sh_gu[:, 1, f * P:(f + 1) * P], rhs, start=True, stop=True
                             ).then_inc(sh_made, 1)

                def shared_down(c, n):
                    after(pe, shared_hid_ready, c * 2 + 2)
                    after(pe, pY_taken, n - 1)
                    if isinstance(c, int) and c == 0:
                        pe.wait_ge(exp_ready, 1)
                    for b in range(NB):
                        for f in range(2):
                            ins = X.matmul(pY[:, b * P:(b + 1) * P], shs[:, f, b * P:(b + 1) * P], sh_dn[:, f, :],
                                           start=(f == 0), stop=(f == 1))
                    ins.then_inc(pY_made, 1)

                def bias_sum(c):
                    pe.wait_ge(selscore_ready, 1)
                    pe.wait_ge(pY_taken, 7 + c)
                    for b in range(NB):
                        ins = X.matmul(pY[:, b * P:(b + 1) * P], selscore[:, b * P:(b + 1) * P], down_b[:, c, :],
                                       start=True, stop=True)
                    ins.then_inc(pY_made, 1)

                def total(j):
                    after(pe, count_ready, j + 1)
                    X.matmul(pU[1][:, 0:1], segones[:, :], cnt[:, 0:1], start=True, stop=True).then_inc(total_ready, 1)

                def sums():
                    pe.wait_ge(count_ready, NBITS + 1)
                    X.matmul(pU[1][:, 0:2], segones[:, :], cnt[:, 0:2], start=True, stop=True)
                    X.matmul(pU[1][:, 2:4], seglow[:, :], cnt[:, 0:2], start=True, stop=True).then_inc(total_ready, 1)

                def offsets():
                    pe.wait_ge(count_ready, NBITS + 2)
                    X.matmul(pU[1][:, 4:5], seglow[:, :], cnt[:, 2:3], start=True, stop=True).then_inc(total_ready, 1)

                def turn_slots():
                    pe.wait_ge(slot_ready, 1)
                    pe.wait_ge(shs_ready, 13)
                    for b in range(NB):
                        X.transpose(pG[0][:, b * P:(b + 1) * P], gt[:, b * P:(b + 1) * P], ident[:, :])
                        ins = X.transpose(pG[1][:, b * P:(b + 1) * P], score[:, b * P:(b + 1) * P], ident[:, :])
                    ins.then_inc(slotT_ready, 1)

                def list_half(half):
                    pe.wait_ge(onehot_ready, half + 1)
                    for t in range(NT // 2):
                        for g in range(E // 4):
                            c = t * E + 4 * g
                            ins = X.matmul(pU[1][:, 64 * g:64 * g + 64],
                                           one_a[:, c // 4].rearrange("p s e -> p (s e)"),
                                           one_b[:, c // 4].rearrange("p s e -> p (s e)"),
                                           start=(half == 0 and t == 0 and g == 0),
                                           stop=(half == 1 and t == NT // 2 - 1), skip_group_check=True)
                    ins.then_inc(list_ready if half else onehot_used, 1)

                def spread_list():
                    pe.wait_ge(list_used, 1)
                    pe.wait_ge(shs_ready, 14)
                    pe.wait_ge(shu_ready, 14)
                    for e4 in range(4):
                        for c in range(4):
                            ins = X.matmul((pG + pU)[e4][32 * c:32 * c + 32, 0:16],
                                           ident[:, :].rearrange("p (a e) -> p e a", e=4)[:, e4],
                                           list_ab[:, :, :].rearrange("p g (q c) -> p c g q", c=4)[:, c],
                                           start=True, stop=True, tile_position=(0, 32 * c))
                    ins.then_inc(idx_made, 1)

                def turn_x(e, s):
                    after(pe, gathered[s % 2], e_half(e, s) * 16 * NB + 16 * NB)
                    after(pe, y_ready, e - 1 + Y0)
                    for b in range(NB):
                        ins = X.transpose(pY[:, b * P:(b + 1) * P], xg[:, s % 2, b, 0:D], ident[:, :])
                    ins.then_inc(xT_made, 1)

                def e_half(e, s):
                    return e // 2 if isinstance(e, int) else eh[0] + s // 2

                eh = [0]

                def expert_step(e, s, f):
                    if f == 0:
                        after(pe, xT_ready, e + 1)
                        after(pe, w_loaded[s % 2], e_half(e, s) * 32 + 32)
                    after(pe, hid_ready, e * NF + f - 1 + HID0)
                    rhs = xinT[:, s % 2, :]
                    X.matmul(pG[f % 2][:, :], wx[:, s % 2, 0, f * P:(f + 1) * P], rhs, start=True, stop=True)
                    X.matmul(pU[f % 2][:, :], wx[:, s % 2, 1, f * P:(f + 1) * P], rhs, start=True, stop=True
                             ).then_inc(gu_made, 1)

                def expert_down(e, s, more):
                    after(pe, hid_ready, e * NF + NF + HID0)
                    after(pe, xT_ready, e + 2 if more else e + 1)
                    after(pe, y_ready, e + Y0)
                    for b in range(NB):
                        for f in range(NF):
                            ins = X.matmul(pY[:, b * P:(b + 1) * P], hid[:, f, b * P:(b + 1) * P],
                                           wx[:, s % 2, 2, f * P:(f + 1) * P], start=(f == 0), stop=(f == NF - 1))
                    ins.then_inc(y_made, 1)

                def pass_(p, searching=False, listing=False, experts=False, finish=True):
                    if experts and not isinstance(p, int):
                        eh[0] = p * 2 - 8
                    c = p + 1
                    for i in range(DK):
                        e = p * EP - 4 * EP + i // 2
                        s, f = i // 2, 2 * (i % 2)
                        if experts:
                            expert_step(e, s, f)
                            expert_step(e, s, f + 1)
                        if i == 0:
                            proj("R", MIX_R, c, (taken["F"], (p - 2) * NF + NF + F0_), (taken["C"], c))
                            if finish:
                                var(p - 1)
                        if i == 1:
                            proj("V", MIX_V, c, (taken["R"], c + 1))
                            proj("K", MIX_K, c, *([(taken["VAR"], p)] if finish else [(taken["G"], c)]))
                            if listing:
                                sums()
                            if searching:
                                total(p * PER)
                            if not experts:
                                shared_up(p, 0, 0)
                            open_o(p)
                            if searching:
                                total(p * PER + SEARCH[1][0])
                            add_o(p, 0)
                        if experts and i % 2 == 1:
                            turn_x(e + 1, s + 1)
                        if i == 2:
                            proj("A", MIX_W, c, (taken["K"], c + 1))
                            if listing:
                                turn_slots()
                                lora_out(c)
                                w_out(p - 1, (taken["A"], c + 1))
                            if not experts:
                                shared_up(p, 0, 1)
                        if i == 3 and not listing:
                            lora_out(c)
                            if finish:
                                w_out(p - 1, (taken["A"], c + 1))
                        if i == 4:
                            if not listing:
                                own(c)
                            proj("G", MIX_G, c, (taken["WO"], p) if finish else (taken["A"], c + 1))
                            if listing:
                                turn_h2(p - 1, (taken["C"], c + 1))
                            elif not experts:
                                shared_down(p * 2, p * 2 + 1)
                        if i == 5:
                            if not experts:
                                shared_up(p, 1, 0)
                            if finish and not listing:
                                turn_h2(p - 1, (taken["C"], c + 1))
                        if i == 6 and not experts:
                            shared_up(p, 1, 1)
                        if i == (7 if experts else 6) and finish and not listing:
                            ff1(p - 1, 0, (taken["G"], c + 1))
                            ff1(p - 1, 1)
                        if experts and i % 2 == 1:
                            if i < 7:
                                add_o(p, i)
                            expert_down(e, s, True)
                        if i == 7:
                            if finish and not listing:
                                ff1(p - 1, 2)
                            if searching:
                                total(p * PER + SEARCH[7][0])
                            if finish and not listing:
                                ff1(p - 1, 3)
                        if searching and 1 < i < 7:
                            total(p * PER + SEARCH[i][0])
                        if i and not (experts and i % 2 == 1 and i < 7):
                            add_o(p, i)
                        if searching and i == 1:
                            total(p * PER + SEARCH[1][1])
                        if listing and i == 1:
                            offsets()
                        if i == 7:
                            if not experts:
                                shared_down(p * 2 + 1, 16 if listing else p * 2 + 2)
                            if searching:
                                total(p * PER + SEARCH[7][1])
                            if finish and not listing:
                                ff2(p - 1)
                        if listing and i == 3:
                            own(c)
                            shared_down(p * 2, p * 2 + 1)
                            bias_sum(0)
                            bias_sum(1)
                            list_half(0)
                        if listing and i == 6:
                            bias_sum(7)
                        if listing and i == 4:
                            bias_sum(2)
                            ff1(p - 1, 0, (taken["G"], c + 1))
                            for k in range(1, NF):
                                bias_sum(2 + k)
                                ff1(p - 1, k)
                            list_half(1)
                            bias_sum(6)
                            spread_list()
                            ff2(p - 1)

                def last_pass(p):
                    for i in range(DK):
                        e = p * EP - 4 * EP + i // 2
                        s, f = i // 2, 2 * (i % 2)
                        c = p - 1 + i // 4
                        expert_step(e, s, f)
                        expert_step(e, s, f + 1)
                        if i % 4 == 0:
                            var(c)
                        if i % 2 == 1 and i < 7:
                            turn_x(e + 1, s + 1)
                        if i == 1:
                            open_o(p)
                        if i % 4 == 3:
                            turn_h2(c, (taken["F"], c * NF + F0_))
                        for k in ((), (0, 1, 2, 3), (4, 5), (6, 7))[i] if i < 4 else ():
                            add_o(p, k)
                        if i in (1, 6):
                            w_out(c, (taken["VAR"], c + 1))
                        if i % 4 == 3:
                            ff1(c, 0, (taken["WO"], c + 1))
                            ff1(c, 1)
                        if i % 2 == 1:
                            expert_down(e, s, i < 7)
                        if i % 4 == 3:
                            ff1(c, 2)
                            ff1(c, 3)
                            ff2(c)

                def turn_rows(s):
                    pe.wait_ge(xn_ready, NB * (s + 1))
                    if s >= 2:
                        pe.wait_ge(xnT_ready, s - 1)
                    for b in range(NB):
                        ins = X.transpose(pG[s % 2][:, b * P:(b + 1) * P], xa[:, NB * s + b, 0:D], ident[:, :])
                    ins.then_inc(xnT_made, 1)
                    pe.wait_ge(hrow_ready, NB * (s + 1))
                    if s >= 2:
                        pe.wait_ge(hT_ready, s - 1)
                    for b in range(NB):
                        ins = X.transpose(pU[s % 2][:, b * P:(b + 1) * P], hrow[:, NB * s + b, :], ident[:, :])
                    ins.then_inc(hT_made, 1)

                pe.wait_ge(first_loaded, 16 * NFIRST)
                X.matmul(pY[0:2, 0:2], ident[:, 0:2], ident[:, 0:2], start=True, stop=True).then_inc(y_made, YM0)
                turn_rows(0)
                turn_rows(1)
                pe.wait_ge(consts_loaded, 16 * (len(const_loads) - NFIRST))
                proj("V", MIX_V, 0, mixed=1)
                for t in range(2, 6):
                    turn_rows(t)
                proj("R", MIX_R, 0, (taken["V"], 1), mixed=2)
                proj("K", MIX_K, 0, mixed=3)
                turn_rows(6)
                turn_rows(7)
                proj("A", MIX_W, 0, (taken["K"], 1))

                def logits(t0, t1):
                    pe.wait_ge(gate_ready, 1)
                    for t in range(t0, t1):
                        pe.wait_ge(xnT_ready, t + 1)
                        ins = X.matmul(pY[:, :], gate_pad[:, t, :], xnT[:, t, :], start=(t == 0), stop=(t == NSEG - 1))
                    return ins

                logits(0, NSEG // 2)
                lora_out(0, (taken["R"], 1))
                logits(NSEG // 2, NSEG).then_inc(logits_ready, 1)
                own(0)
                proj("G", MIX_G, 0, (taken["A"], 1))
                pe.wait_ge(hT_ready, NSEG)
                pe.wait_ge(bias_loaded, 16 * NSEG)
                pass_(0, searching=True, finish=False)
                with pe.Fori(1, 3) as p:
                    pass_(p, searching=True)
                pass_(LIST_PASS, listing=True)
                pe.wait_ge(pY_taken, 16)
                turn_x(0, 0)
                with pe.Fori(4, 7) as p:
                    pass_(p, experts=True)
                last_pass(LAST)

        fin_loaded = [sem(f"fin_loaded{q}") for q in range(4)]
        sum_ready = sem("sum_ready")
        act_ready = sem("act_ready")
        prod_ready = sem("prod_ready")
        fin_ready = sem("fin_ready")
        out_stored = sem("out_stored")
        share = xnT[:, :, :].rearrange("p s (b c) -> p s b c", b=NB)
        s_all = hT[:, :, 0:SEG].rearrange("p s (b c) -> p s b c", b=NB)
        x_all = xa[:, :, 0:D].rearrange("p (s b) c -> p s b c", b=NB)
        m_all = moe.rearrange("p (s b) c -> p s b c", b=NB)
        with nc.Block() as block:
            @block.sync
            def _(sp):
                view = lambda t: t.rearrange("(q i p) c -> q p i c", p=P, q=4)
                for q in range(4):
                    sp.dma_start(moe[:, QT * q:QT * q + QT, :], view(moe_sum[:, :])[q]).then_inc(fin_loaded[q], 16)
                for q in range(4):
                    sp.wait_ge(fin_ready, 2 * q + 2)
                    sp.dma_start(view(out)[q], moe[:, QT * q:QT * q + QT, :]).then_inc(out_stored, 16)
                sp.wait_ge(out_stored, 64)

            @block.vector
            def _(v):
                for c in range(NSEG + 1):
                    if c < NSEG:
                        v.wait_ge(fin_loaded[c // 2], 16)
                        nc.vector.tensor_tensor(m_all[:, c], m_all[:, c], share[:, c], ALU.add).then_inc(sum_ready, 1)
                    if c:
                        v.wait_ge(act_ready, c)
                        nc.vector.tensor_tensor(s_all[:, c - 1], s_all[:, c - 1], share[:, c - 1],
                                                ALU.mult).then_inc(prod_ready, 1)

            @block.gpsimd
            def _(pool):
                for c in range(NSEG):
                    pool.wait_ge(prod_ready, c + 1)
                    nc.gpsimd.tensor_tensor(m_all[:, c], x_all[:, c], s_all[:, c], ALU.add).then_inc(fin_ready, 1)

            @block.scalar
            def _(act):
                for c in range(NSEG):
                    act.wait_ge(sum_ready, c + 1)
                    nc.scalar.activation(share[:, c], m_all[:, c], ACT.Silu).then_inc(act_ready, 1)


def shape_constants():
    f = np.float32
    k = np.arange(P)
    same_head = (k[:, None] // DK == k[None, :] // DK)
    c = {"ident": np.eye(P), "headones": same_head, "headmean": same_head / DK,
         "center": np.eye(P) - same_head / DK}
    c["selc"] = same_head[:, None, :] * ((k[None, None, :] % DK == np.arange(DK)[None, :, None]) - 1.0 / DK)
    same_expert = (k[:, None] % E == k[None, :] % E)
    c["segones"] = same_expert
    c["seglow"] = same_expert & (k[:, None] // E < k[None, :] // E)
    c = {n: np.ascontiguousarray(a, f) for n, a in c.items()}
    c["bits"] = np.ascontiguousarray(np.broadcast_to(1 << np.arange(NBITS - 1, -1, -1), (P, NBITS)), np.int32)
    c["iota"] = np.ascontiguousarray(np.broadcast_to(np.repeat(np.arange(SHIGH), 4), (P, 4 * SHIGH)), np.float16)
    c["own4"] = np.ascontiguousarray(k[:, None] % 4 == np.arange(4)[None, :], f)
    blk, seg = np.meshgrid(np.arange(NB), np.arange(NSEG), indexing="ij")
    base = np.repeat((seg * SEG + blk * P).ravel(), E)
    c["tokval"] = (base[None, :] + k[:, None] - TOK // 2).astype(np.float16)
    return c


def kernel(**inputs):
    import concourse.bacc as bacc
    from concourse.bass_utils import run_bass_kernel_spmd

    a = {n: np.asarray(x) for n, x in inputs.items()}
    L = {n[len("L0_attn_"):]: x for n, x in a.items() if n.startswith("L0_attn_")}
    M = {n[len("L0_ffn_"):]: x for n, x in a.items() if n.startswith("L0_ffn_")}
    f = np.float32
    eps = np.full((P,), EPS_GN, f)
    arrays = shape_constants()
    arrays["x"] = L["x"].reshape(TOK, D)
    arrays["vec"] = np.stack([L["ln1_w"], L["mu_r"], L["mu_k"], L["mu_v"], L["mu_w"], L["mu_g"], L["w0"],
                              L["u"].reshape(P), L["gn_w"].reshape(P), L["gn_b"].reshape(P), L["ln2_w"], eps], 1)
    arrays["w_rkvg"] = np.stack([L["Wr"], L["Wk"], L["Wv"], L["Wg"]], 1)
    arrays["w_a"], arrays["w_b"], arrays["w_o"] = L["wA"], L["wB"], L["Wo"]
    arrays["w_f1"] = L["ffn_w1"]
    arrays["w_f2"] = L["ffn_w2"].reshape(NF, P, D).transpose(1, 0, 2)
    arrays["gate"] = M["gate_w"].T
    arrays["sh_gu"] = np.stack([M["sh_gate_w"].T, M["sh_up_w"].T], 1)
    arrays["sh_dn"] = M["sh_down_w"].T.reshape(2, P, D).transpose(1, 0, 2)
    arrays["down_b"] = M["down_b"]
    arrays["ex_bias"] = np.stack([M["gb"].reshape(E * NF, P).T, M["up_b"].reshape(E * NF, P).T], 1)
    arrays["ex_gu"] = np.stack([M["gw"].transpose(0, 2, 1), M["up_w"].transpose(0, 2, 1)], 2)
    arrays["ex_dn"] = M["down_w"].transpose(0, 2, 1).reshape(E, NF, P, D).transpose(0, 2, 1, 3).reshape(E, P, FF)
    arrays = {n: np.ascontiguousarray(x) for n, x in arrays.items()}

    nc = bacc.Bacc("TRN2", target_bir_lowering=False, num_devices=1)
    d = {n: nc.dram_tensor("in_" + n, x.shape, mybir.dt.from_np(x.dtype), kind="ExternalInput").ap()
         for n, x in arrays.items()}
    out = nc.dram_tensor("out", (TOK, D), F32, kind="ExternalOutput").ap()
    build(nc, d, out)
    r = run_bass_kernel_spmd(nc, [{"in_" + n: x for n, x in arrays.items()}], core_ids=[0])
    return r.results[0]["out"].reshape(B, T, D)
```
